# Optimizing a Trainium2 kernel written in Bass

```python
import numpy as np
import jax
import jax.numpy as jnp

def _softmax(x, axis=-1):
    return jax.nn.softmax(x, axis=axis)

def _gelu(x):
    return jax.nn.gelu(x, approximate=True)

def _silu(x):
    return jax.nn.silu(x)

def _sigmoid(x):
    return jax.nn.sigmoid(x)

def _layernorm(x, axis=-1, eps=1e-05):
    m = jnp.mean(x, axis=axis, keepdims=True)
    v = jnp.var(x, axis=axis, keepdims=True)
    return (x - m) / jnp.sqrt(v + eps)

def _scatter_add(tgt, idx, src, axis=0):
    return tgt.at[idx].add(src)

def _segment_sum(src, seg, n):
    return jax.ops.segment_sum(src, seg, n)
kernel_name = 'mk_xattn_ffn_d2_seqx_r8_0dfbd4'

def setup_inputs(seed: int=0):
    np.random.seed(seed)
    _w = jnp.asarray

    def _rec_inputs():
        import jax
        import jax.numpy as jnp
        _rk = jax.random.key(seed)
        x = -7.109e-05 + 0.9999 * jax.random.normal(jax.random.fold_in(_rk, 1), (4, 256, 256), jnp.float32)
        _lenS = 256 - jax.random.randint(jax.random.fold_in(_rk, 7), (4,), 0, max(1, 256 // 4) + 1, jnp.int32)
        _lenS2 = 256 - jax.random.randint(jax.random.fold_in(_rk, 8), (4,), 0, max(1, 256 // 4) + 1, jnp.int32)
        _ctx_2048P = jax.random.normal(jax.random.fold_in(_rk, 11), (4, 16, 256), jnp.float32)
        _ctx_2048c = jax.random.dirichlet(jax.random.fold_in(_rk, 511), 0.3 * jnp.ones((16,), jnp.float32), (4, 256))
        _ctx_2048t = jnp.einsum('bsk,bkd->bsd', _ctx_2048c, _ctx_2048P)
        _ctx_2048t = _ctx_2048t * jax.lax.rsqrt(jnp.mean(jnp.square(_ctx_2048t)) + 1e-12) * 0.953939
        ctx_2048 = -3.05549e-07 + 0.0199987 * (_ctx_2048t + 0.3 * jax.random.normal(jax.random.fold_in(_rk, 611), (4, 256, 256), jnp.float32))
        return (x, ctx_2048)
    x, ctx_2048 = _rec_inputs()

    def _L0_xattn_setup():
        import jax, jax.numpy as jnp
        import numpy as np
        FP8_MAX = 448.0
        ACT_EPS = 0.0001
        W_EPS = 1e-06
        BLK = 128

        def quant_dequant_act_1x128(x):
            E, M, K = x.shape
            xb = x.reshape(E, M, K // BLK, BLK)
            amax = jnp.max(jnp.abs(xb), axis=-1, keepdims=True)
            safe = jnp.maximum(amax, ACT_EPS)
            q = (xb * (FP8_MAX / safe)).astype(jnp.float8_e4m3fn)
            return (q.astype(jnp.float32) * (safe / FP8_MAX)).reshape(E, M, K)

        def quant_dequant_weight_128x128(w):
            E, N, K = w.shape
            wb = w.reshape(E, N // BLK, BLK, K // BLK, BLK)
            amax = jnp.max(jnp.abs(wb), axis=(2, 4), keepdims=True)
            safe = jnp.maximum(amax, W_EPS)
            q = (wb * (FP8_MAX / safe)).astype(jnp.float8_e4m3fn)
            return (q.astype(jnp.float32) * (safe / FP8_MAX)).reshape(E, N, K)
        key = jax.random.key(seed)
        kx, kw = jax.random.split(key)
        E, M, K, N = (8, 512, 256, 256)
        x = jax.random.normal(kx, (E, M, K), dtype=jnp.float32)
        weight = jax.random.normal(kw, (E, N, K), dtype=jnp.float32) * 0.02
        return {'x': x, 'weight': weight}
    _L0_xattn_all = _L0_xattn_setup()
    _L0_xattn_in = {k: v for k, v in _L0_xattn_all.items() if k in ()}
    del _L0_xattn_all

    def _L0_ffn_setup():
        import jax, jax.numpy as jnp
        import numpy as np
        B, S, H = (1, 64, 256)
        I = 192
        E = 32
        K = 4
        SCALE = 1.8
        key = jax.random.key(seed)
        ks = jax.random.split(key, 9)
        init = lambda k, shape: jax.random.normal(k, shape, jnp.float32) * (1.0 / np.sqrt(shape[-1]))
        return {'x': jax.random.normal(ks[0], (B, S, H), jnp.float32), 'router_w': init(ks[1], (E, H)), 'router_b': jnp.zeros((E,), jnp.float32), 'gate_w': init(ks[2], (E, I, H)), 'up_w': init(ks[3], (E, I, H)), 'down_w': init(ks[4], (E, H, I)), 'shared_gate_w': init(ks[5], (I, H)), 'shared_up_w': init(ks[6], (I, H)), 'shared_down_w': init(ks[7], (H, I))}
    _L0_ffn_all = _L0_ffn_setup()
    _L0_ffn_in = {k: v for k, v in _L0_ffn_all.items() if k in ('router_w', 'router_b', 'gate_w', 'up_w', 'down_w', 'shared_gate_w', 'shared_up_w', 'shared_down_w')}
    del _L0_ffn_all

    def _L1_xattn_setup():
        import jax, jax.numpy as jnp
        import numpy as np
        N_HEAD = 8
        key = jax.random.key(seed)
        k1, k2, k3 = jax.random.split(key, 3)
        B, D, L = (4, 128, 256)
        q = jax.random.normal(k1, (B, D, L), dtype=jnp.float32)
        k = jax.random.normal(k2, (B, D, L), dtype=jnp.float32)
        v = jax.random.normal(k3, (B, D, L), dtype=jnp.float32)
        gamma = jnp.ones((), dtype=jnp.float32)
        return {'q': q, 'k': k, 'v': v, 'gamma': gamma}
    _L1_xattn_all = _L1_xattn_setup()
    _L1_xattn_in = {k: v for k, v in _L1_xattn_all.items() if k in ('gamma',)}
    del _L1_xattn_all

    def _L1_ffn_setup():
        import jax, jax.numpy as jnp
        import numpy as np
        E = 8
        K = 2
        C = 256
        I = 176
        IS = I * 2
        B, T = (2, 256)
        key = jax.random.key(seed)
        ks = jax.random.split(key, 9)
        s = 0.02
        return {'x': jax.random.normal(ks[0], (B, T, C), dtype=jnp.float32), 'gate_w': jax.random.normal(ks[1], (E, C), dtype=jnp.float32) * s, 'w1': jax.random.normal(ks[2], (E, I, C), dtype=jnp.float32) * s, 'w2': jax.random.normal(ks[3], (E, I, C), dtype=jnp.float32) * s, 'w3': jax.random.normal(ks[4], (E, C, I), dtype=jnp.float32) * s, 'sw1': jax.random.normal(ks[5], (IS, C), dtype=jnp.float32) * s, 'sw2': jax.random.normal(ks[6], (IS, C), dtype=jnp.float32) * s, 'sw3': jax.random.normal(ks[7], (C, IS), dtype=jnp.float32) * s}
    _L1_ffn_all = _L1_ffn_setup()
    _L1_ffn_in = {k: v for k, v in _L1_ffn_all.items() if k in ('gate_w', 'w1', 'w2', 'w3', 'sw1', 'sw2', 'sw3')}
    del _L1_ffn_all
    return {'x': x, 'ctx_2048': ctx_2048, 'L0_ffn_router_w': _L0_ffn_in['router_w'], 'L0_ffn_router_b': _L0_ffn_in['router_b'], 'L0_ffn_gate_w': _L0_ffn_in['gate_w'], 'L0_ffn_up_w': _L0_ffn_in['up_w'], 'L0_ffn_down_w': _L0_ffn_in['down_w'], 'L0_ffn_shared_gate_w': _L0_ffn_in['shared_gate_w'], 'L0_ffn_shared_up_w': _L0_ffn_in['shared_up_w'], 'L0_ffn_shared_down_w': _L0_ffn_in['shared_down_w'], 'L1_xattn_gamma': _L1_xattn_in['gamma'], 'L1_ffn_gate_w': _L1_ffn_in['gate_w'], 'L1_ffn_w1': _L1_ffn_in['w1'], 'L1_ffn_w2': _L1_ffn_in['w2'], 'L1_ffn_w3': _L1_ffn_in['w3'], 'L1_ffn_sw1': _L1_ffn_in['sw1'], 'L1_ffn_sw2': _L1_ffn_in['sw2'], 'L1_ffn_sw3': _L1_ffn_in['sw3']}

def reference(x, ctx_2048, L0_ffn_router_w, L0_ffn_router_b, L0_ffn_gate_w, L0_ffn_up_w, L0_ffn_down_w, L0_ffn_shared_gate_w, L0_ffn_shared_up_w, L0_ffn_shared_down_w, L1_xattn_gamma, L1_ffn_gate_w, L1_ffn_w1, L1_ffn_w2, L1_ffn_w3, L1_ffn_sw1, L1_ffn_sw2, L1_ffn_sw3):
    import jax
    import jax.numpy as jnp

    def _L0_xattn_ref(x, weight):
        import jax, jax.numpy as jnp
        import numpy as np
        FP8_MAX = 448.0
        ACT_EPS = 0.0001
        W_EPS = 1e-06
        BLK = 128

        def quant_dequant_act_1x128(x):
            E, M, K = x.shape
            xb = x.reshape(E, M, K // BLK, BLK)
            amax = jnp.max(jnp.abs(xb), axis=-1, keepdims=True)
            safe = jnp.maximum(amax, ACT_EPS)
            q = (xb * (FP8_MAX / safe)).astype(jnp.float8_e4m3fn)
            return (q.astype(jnp.float32) * (safe / FP8_MAX)).reshape(E, M, K)

        def quant_dequant_weight_128x128(w):
            E, N, K = w.shape
            wb = w.reshape(E, N // BLK, BLK, K // BLK, BLK)
            amax = jnp.max(jnp.abs(wb), axis=(2, 4), keepdims=True)
            safe = jnp.maximum(amax, W_EPS)
            q = (wb * (FP8_MAX / safe)).astype(jnp.float8_e4m3fn)
            return (q.astype(jnp.float32) * (safe / FP8_MAX)).reshape(E, N, K)
        xq = quant_dequant_act_1x128(x)
        wq = quant_dequant_weight_128x128(weight)
        return jnp.einsum('emk,enk->emn', xq, wq)

    def _L0_ffn_ref(x, router_w, router_b, gate_w, up_w, down_w, shared_gate_w, shared_up_w, shared_down_w):
        import jax, jax.numpy as jnp
        import numpy as np
        B, S, H = (1, 64, 256)
        I = 192
        E = 32
        K = 4
        SCALE = 1.8
        b, s, h = x.shape
        xf = x.reshape(-1, h).astype(jnp.float32)
        logits = xf @ router_w.T + router_b
        top_vals, top_idx = jax.lax.top_k(logits, K)
        rw = jax.nn.softmax(top_vals, axis=-1) * SCALE
        combine = jnp.einsum('tke,tk->te', jax.nn.one_hot(top_idx, E, dtype=xf.dtype), rw)
        g = jax.nn.silu(jnp.einsum('th,eih->tei', xf, gate_w))
        u = jnp.einsum('th,eih->tei', xf, up_w)
        routed = jnp.einsum('tei,ehi,te->th', g * u, down_w, combine)
        sg = jax.nn.silu(xf @ shared_gate_w.T)
        su = xf @ shared_up_w.T
        shared = sg * su @ shared_down_w.T
        return (routed + shared).reshape(b, s, h)

    def _L1_xattn_ref(q, k, v, gamma):
        import jax, jax.numpy as jnp
        import numpy as np
        N_HEAD = 8
        B, Dq, Lq = q.shape
        Dv, Lk = (v.shape[-2], v.shape[-1])
        h = N_HEAD
        dq = Dq // h
        dv = Dv // h
        qh = q.reshape(B, h, dq, Lq)
        kh = k.reshape(B, h, dq, Lk)
        vh = v.reshape(B, h, dv, Lk)
        scale = 1.0 / jnp.sqrt(jnp.asarray(dq, dtype=q.dtype))
        qk = jnp.einsum('bhdq,bhdl->bhql', qh, kh) * scale
        sm = jax.nn.softmax(qk, axis=-1)
        ret = jnp.einsum('bhql,bhdl->bhdq', sm, vh)
        ret = ret.reshape(B, Dv, Lq)
        return gamma * ret

    def _L1_ffn_ref(x, gate_w, w1, w2, w3, sw1, sw2, sw3):
        import jax, jax.numpy as jnp
        import numpy as np
        E = 8
        K = 2
        C = 256
        I = 176
        IS = I * 2
        B, T = (2, 256)
        Bq, Tq, Cq = x.shape
        xf = x.reshape(-1, Cq)
        logits = xf @ gate_w.T
        probs = jax.nn.softmax(logits.astype(jnp.float32), axis=-1)
        topk_p, topk_i = jax.lax.top_k(probs, K)
        comb = (jax.nn.one_hot(topk_i, E, dtype=jnp.float32) * topk_p[..., None]).sum(axis=1).astype(x.dtype)
        h1 = jnp.einsum('nc,eic->eni', xf, w1)
        h2 = jnp.einsum('nc,eic->eni', xf, w2)
        h = jax.nn.silu(h1) * h2
        eo = jnp.einsum('eni,eci->enc', h, w3)
        y = jnp.einsum('enc,ne->nc', eo, comb).reshape(Bq, Tq, Cq)
        sh = jax.nn.silu(xf @ sw1.T) * (xf @ sw2.T) @ sw3.T
        return y + sh.reshape(Bq, Tq, Cq)
    x = x + _L0_xattn_ref(_layernorm(x, axis=-1), ctx_2048)
    x = x + _L0_ffn_ref(_layernorm(x, axis=-1), L0_ffn_router_w, L0_ffn_router_b, L0_ffn_gate_w, L0_ffn_up_w, L0_ffn_down_w, L0_ffn_shared_gate_w, L0_ffn_shared_up_w, L0_ffn_shared_down_w)
    x = x + _L1_xattn_ref(_layernorm(x, axis=-1), ctx_2048, ctx_2048, L1_xattn_gamma)
    x = x + _L1_ffn_ref(_layernorm(x, axis=-1), L1_ffn_gate_w, L1_ffn_w1, L1_ffn_w2, L1_ffn_w3, L1_ffn_sw1, L1_ffn_sw2, L1_ffn_sw3)
    return x

_drawn_inputs = setup_inputs


def setup_inputs(seed=0):
    import zlib

    import numpy as np

    out = dict(_drawn_inputs(seed))
    spreads = {'L0_ffn_router_b': (0.0, 0.1)}
    factors = {'L1_ffn_gate_w': 8.0,
     'L1_ffn_w1': 8.0,
     'L1_ffn_w2': 8.0,
     'L1_ffn_w3': 8.0,
     'L1_ffn_sw1': 3.881,
     'L1_ffn_sw2': 3.854,
     'L1_ffn_sw3': 3.861}
    for name, (base, spread) in spreads.items():
        noise = np.random.default_rng([zlib.crc32(name.encode()), seed]).standard_normal(out[name].shape)
        drawn = base * np.exp(spread * noise) if base else spread * noise
        out[name] = jnp.asarray(drawn.astype(out[name].dtype))
    for name, factor in factors.items():
        out[name] = (out[name] * factor).astype(out[name].dtype)
    return out
```

```python
from contextlib import ExitStack

import numpy as np
import concourse.bass as bass
from concourse import mybir

ALU = mybir.AluOpType
ACT = mybir.ActivationFunctionType
AX = mybir.AxisListType
F32 = mybir.dt.float32
F16 = mybir.dt.float16
BF16 = mybir.dt.bfloat16
I32 = mybir.dt.int32
U32 = mybir.dt.uint32

P = 128
LN_EPS = 1e-5
FP8_MAX = 448.0
ACT_EPS = 1e-4
W_EPS = 1e-6
ROUTED_SCALE = 1.8
UNROLL = 4
EARLY = 9
HEAD = 32


class Moe:

    def __init__(self, name, E, K, half, shared, n_tok):
        self.name, self.E, self.K, self.J, self.S = name, E, K, half, shared
        most = (n_tok * K + (P - 1) * E) // P
        self.tiles = -(-most // UNROLL) * UNROLL
        self.gu = 2 * 2 * 2 * half


def mk_xattn_ffn(nc, x, ctx, ctxT, router_w0, router_b0, w_gu0, w_dn0, gamma, router_w1, w_gu1, w_dn1, out):
    NT, _, H = x.shape
    C = H // P
    n_tok = NT * P
    NB = ctx.shape[0]
    HPT = P // HEAD
    SCALE = float(HEAD) ** -0.5
    L0 = Moe("m0", router_w0.shape[2], 4, w_dn0.shape[0], 1, n_tok)
    L1 = Moe("m1", router_w1.shape[2], 2, w_dn1.shape[0], 2, n_tok)
    for L in (L0, L1):
        L.stride = L.gu + 2 * H

    with ExitStack() as es:
        def sb(name, shape, dt=F32):
            return es.enter_context(nc.sbuf_tensor(name, shape, dt))

        def sem(name):
            return es.enter_context(nc.semaphore(name))

        bank = [es.enter_context(nc.psum_tensor(f"bank{i}", [P, 512], F32)) for i in range(8)]

        W_COLS = (L0.S + L0.E) * L0.stride
        arena = sb("arena", [P, W_COLS])
        x_sb = sb("x_sb", [P, NT, H])
        xn = sb("xn", [P, NT, H])
        ident = sb("ident", [P, P])
        ident16 = sb("ident16", [P, P], BF16)
        tri16 = sb("tri16", [P, P], BF16)
        tri_in16 = sb("tri_in16", [P, P], BF16)
        ones16 = sb("ones16", [P, P], BF16)
        ones32 = sb("ones32", [P, P])
        iota16 = sb("iota16", [P, P], F16)
        iota_e = sb("iota_e", [P, L0.E])
        thr = sb("thr", [P, NT])
        tokid = sb("tokid", [P, NT])
        gamma_sb = sb("gamma_sb", [P, 1])
        rw0 = sb("rw0", [P, C, L0.E])
        rb0 = sb("rb0", [1, L0.E])
        rw1 = sb("rw1", [P, C, L1.E])
        xg = sb("xg", [P, UNROLL, H])
        xT = sb("xT", [P, 2, C, P])
        sg = sb("sg", [P, 2, 2 * L0.J])
        up = sb("up", [P, 2, 2 * L0.J])
        hh = sb("hh", [P, 2, 2 * L0.J])
        hT = sb("hT", [P, 2, 2, P])
        ysb = sb("ysb", [P, UNROLL, H])
        gidx = sb("gidx", [P, UNROLL], U32)
        st = sb("st", [P, NT, 6])
        mv = sb("mv", [P, NT, 2])
        ve = sb("ve", [P, NT])
        nt = sb("nt", [P, NT])
        rstd = sb("rstd", [P, NT])
        amc = sb("amc", [P, 16])
        amx = sb("amx", [P, 16])
        col16 = sb("col16", [P, 1])
        diag = sb("diag", [P, 16])
        safe_c = sb("safe_c", [P, 16])
        rin_c = sb("rin_c", [P, 16])
        rin_x = sb("rin_x", [P, 16])
        dq = sb("dq", [P, NT, C, C])
        small = {L0.name: {}, L1.name: {}}

        def routed(name, shape_of, dt=F32, rows=P):
            flat = sb(name, [rows, max(int(np.prod(shape_of(L))) for L in (L0, L1))], dt)
            for L in (L0, L1):
                shape = shape_of(L)
                v = flat[:, 0:int(np.prod(shape))]
                small[L.name][name] = v.rearrange("p (t k) -> p t k", t=shape[0]) if len(shape) == 2 else v

        routed("lg", lambda L: (NT, L.E))
        routed("m16", lambda L: (NT, L.E), BF16)
        for n in ("top", "idxf"):
            routed(n, lambda L: (NT, 8))
        routed("idx", lambda L: (NT, 8), U32)
        for n, dt in (("rw", F32), ("slotf", F32), ("tf", F32), ("pf", F32), ("sloti", I32), ("ti", I32), ("pi", I32),
                      ("back", U32)):
            routed(n, lambda L: (NT, L.K), dt)
        for n in ("s1", "s2", "junk"):
            routed(n, lambda L: (NT,))
        for n in ("cnt", "ntc", "endc"):
            routed(n, lambda L: (1,))
        routed("ntr", lambda L: (P,), BF16)
        routed("cmp", lambda L: (L.tiles,), BF16)
        routed("startb", lambda L: (L.E,))
        routed("tab", lambda L: (L.tiles,), U32)
        routed("te", lambda L: (L.tiles,), rows=1)
        routed("etab", lambda L: (L.tiles,), I32, rows=1)
        for n in ("nm", "rsum", "rinv"):
            small[n] = sb("att_" + n, [P, 3, 2])

        def part(at, cols):
            return arena[:, at:at + cols], at + cols

        LATE = 6
        late0 = (W_COLS // L0.stride - LATE) * L0.stride
        at = late0
        v_c, at = part(at, NB * C * H)
        c_c, at = part(at, NB * C * H)
        c_x, at = part(at, NT * H)
        wq, at = part(at, NB * C * H // 2)
        assert at <= W_COLS
        wq = wq.bitcast(BF16).rearrange("p (b k n) -> p b k n", b=NB, k=C)
        v_x = xn[:].rearrange("p t h -> p (t h)")
        qx = ysb[:].rearrange("p s h -> p (s h)").bitcast(BF16)
        xqT = xg[:].rearrange("p s h -> p (s h)").bitcast(BF16).rearrange("p (t k m) -> p t k m", t=NT, k=C)
        RS = {}
        for L, at in ((L0, late0), (L1, 22000)):
            d = {}
            n = NT * L.K * L.E
            d["oh"], at = part(at, n)
            d["pr"], at = part(at, n)
            d["base"], at = part(at, NT * L.E)
            d["pos1"], at = part(at, NT * L.K * P // 2)
            d["til1"], at = part(at, NT * L.K * L.tiles // 2)
            d["xT"], at = part(at, NT * H)
            d["xT"] = d["xT"].rearrange("p (t c m) -> p t c m", t=NT, c=C)
            d["oh"] = d["oh"].rearrange("p (t k e) -> p t k e", t=NT, k=L.K)
            d["pr"] = d["pr"].rearrange("p (t k e) -> p t k e", t=NT, k=L.K)
            d["base"] = d["base"].rearrange("p (t e) -> p t e", t=NT)
            d["pos1"] = d["pos1"].bitcast(F16).rearrange("p (a m) -> p a m", m=P)
            d["til1"] = d["til1"].bitcast(F16).rearrange("p (a m) -> p a m", m=L.tiles)
            assert at <= W_COLS
            RS[L.name] = d
        at = 0
        w1_all, at = part(at, (L1.S + L1.E) * L1.stride)
        k_sb, at = part(at, NB * C * H)
        vT, at = part(at, NB * C * H)
        k_sb = k_sb.rearrange("p (t n) -> p t n", t=NT)
        vT = vT.rearrange("p (b k n) -> p b k n", b=NB, k=C)
        pr_sb, at = part(at, 3 * 2 * H)
        pT_sb, at = part(at, 2 * 2 * H)
        pr_sb = pr_sb.rearrange("p (b q k) -> p b q k", b=3, q=2)
        pT_sb = pT_sb.rearrange("p (b k q) -> p b k q", b=2, k=2)
        assert at <= 22000
        back_rows = {}
        at = 30000
        for L in (L0, L1):
            r, _ = part(at, NT * L.K * H)
            back_rows[L.name] = r.rearrange("p (t k h) -> p t k h", t=NT, k=L.K)
            assert at + NT * L.K * H <= W_COLS

        xn_d = {L.name: nc.dram_tensor(L.name + "_xn", (n_tok, H), F32, kind="Internal").ap() for L in (L0, L1)}
        ys_d = {L.name: nc.dram_tensor(L.name + "_ys", (L.tiles * P, H), F32, kind="Internal").ap() for L in (L0, L1)}

        x_in = [sem(f"x_in{t}") for t in range(NT // 2)]
        ctxT_in, k_in, v_in = sem("ctxT_in"), sem("k_in"), sem("v_in")
        small_in = sem("small_in")
        w_shared, w_early, w_late, w1_in = sem("w_shared"), sem("w_early"), sem("w_late"), sem("w1_in")
        consts = sem("consts")
        consts0 = sem("consts0")
        dve_step = sem("dve_step")
        pool_step = sem("pool_step")
        amc_ready, amcT_done, diag_ready, amb_done = (sem(n) for n in ("amc_ready", "amcT_done", "diag_ready", "amb_done"))
        c_mag, wq_ready, xq_ready, xqT_done, xqT_sb, xp_done, x1_ready = (
            sem(n) for n in ("c_mag", "wq_ready", "xq_ready", "xqT_done", "xqT_sb", "xp_done", "x1_ready"))

        M = {}
        for L in (L0, L1):
            m = {n: sem(f"{L.name}_{n}") for n in (
                "xn_ready xn_stored rt_T rt_Tsb logits exp_in exp_out mask counts ntiles starts "
                "cmp owner table_e onehots tokens table idx_col idx_seen t_done xT_copied g_done "
                "sg_ready h_ready ht_done hT_copied d_done y_copied ").split()}
            m["xg_in"] = [sem(f"{L.name}_xg_in{i}") for i in range(UNROLL)]
            m["y_stored"] = [sem(f"{L.name}_y_stored{i}") for i in range(UNROLL)]
            m["rows_back"] = [sem(f"{L.name}_rows_back{i}") for i in range(NT)]
            m["pass"] = [{n: sem(f"{L.name}_pass{i}_{n}") for n in
                          "g_done evacuated h_ready ht_done hT_copied d_done y_copied added".split()}
                         for i in range(L.S)]
            M[L.name] = m
        x2_ready, q_ready, s_done, nm_ready, p_raw, p_ready, tp_done, pT_ready, av_done, x3_ready = (
            sem(n) for n in ("x2_ready", "q_ready", "s_done", "nm_ready", "p_raw", "p_ready", "tp_done", "pT_ready", "av_done", "x3_ready"))
        out_ready, stored = sem("out_ready"), sem("stored")

        block = es.enter_context(nc.Block())
        nheads = NT * HPT

        def turns(eng, L, turn, early=1):
            n = L.tiles // UNROLL
            for g in range(early):
                turn(g * UNROLL, g, g == 0, False)
            with eng.Fori(early, n - 1) as g:
                turn(g * UNROLL, g, False, False)
            turn((n - 1) * UNROLL, n - 1, False, True)

        @block.sync
        def _(sp):
            for t in range(0, NT, 2):
                sp.dma_start(x_sb[:, t:t + 2, :], x[t:t + 2].rearrange("t p h -> p t h")).then_inc(x_in[t // 2], 16)
            n0 = L0.S + L0.E

            def experts(L, a, b, w_gu, w_dn, done):
                w = arena[:, a * L.stride:b * L.stride].rearrange("p (e c) -> p e c", c=L.stride)
                sp.dma_start(w[:, :, 0:L.gu], w_gu[:, a:b, :]).then_inc(done, 16)
                sp.dma_start(w[0:L.J, :, L.gu:L.stride], w_dn[:, a:b, :]).then_inc(done, 16)

            def store_xn(L):
                m = M[L.name]
                sp.wait_ge(m["xn_ready"], NT)
                sp.dma_start(xn_d[L.name].rearrange("(t p) h -> p t h", p=P), xn[:]).then_inc(m["xn_stored"], 16)

            def store_tiles(L):
                m = M[L.name]

                def turn(base, group, first, last):
                    for j in range(UNROLL):
                        sp.wait_ge(m["y_copied"], base + j + 1)
                        sp.dma_start(ys_d[L.name][bass.ds((base + j) * P, P), :], ysb[:, j, :]).then_inc(m["y_stored"][j], 16)

                turns(sp, L, turn)
                for j in range(UNROLL):
                    sp.wait_ge(m["y_stored"][j], 16 * (L.tiles // UNROLL))

            sp.wait_ge(ctxT_in, 16)
            experts(L0, 0, L0.S, w_gu0, w_dn0, w_shared)
            for a in range(L0.S, n0 - LATE, EARLY):
                experts(L0, a, min(a + EARLY, n0 - LATE), w_gu0, w_dn0, w_early)
            store_xn(L0)
            sp.wait_ge(M["m0"]["table"], 1)
            sp.wait_ge(M["m0"]["pass"][0]["g_done"], NT)
            experts(L0, n0 - LATE, n0, w_gu0, w_dn0, w_late)
            store_tiles(L0)
            sp.wait_ge(M["m0"]["d_done"], L0.tiles)
            sp.dma_start(k_sb, ctx.rearrange("b (k p) n -> p (b k) n", p=P)).then_inc(k_in, 16)
            sp.dma_start(vT, ctxT.rearrange("b (k p) n -> p b k n", p=P)).then_inc(v_in, 16)
            for t in range(NT):
                sp.wait_ge(M["m0"]["rows_back"][t], 16 * L0.K)
            experts(L1, 0, L1.S + L1.E, w_gu1, w_dn1, w1_in)
            store_xn(L1)
            store_tiles(L1)
            for t in range(NT):
                sp.wait_ge(out_ready, t + 1)
                sp.dma_start(out[t], x_sb[:, t, :]).then_inc(stored, 16)
            sp.wait_ge(stored, 16 * NT)

        @block.gpsimd
        def _(pool):
            step = [0]

            def link(ins):
                step[0] += 1
                ins.then_inc(pool_step, 1)
                pool.wait_ge(pool_step, step[0])

            nc.gpsimd.memset(ident[:], 0.0).then_inc(consts0, 1)
            nc.gpsimd.memset(ident16[:], 0.0).then_inc(consts0, 1)
            nc.gpsimd.memset(ones16[:], 1.0).then_inc(consts0, 1)
            nc.gpsimd.memset(ones32[:], 1.0).then_inc(consts0, 1)
            pool.wait_ge(consts0, 4)
            for i in (ident, ident16):
                nc.gpsimd.affine_select(out=i[:], in_=i[:], compare_op=ALU.not_equal, fill=1.0, base=0,
                                        pattern=[[-1, P]], channel_multiplier=1).then_inc(consts, 1)
            nc.gpsimd.affine_select(out=tri16[:], in_=ones16[:], compare_op=ALU.is_gt, fill=0.0, base=0,
                                    pattern=[[1, P]], channel_multiplier=-1).then_inc(consts, 1)
            nc.gpsimd.affine_select(out=tri_in16[:], in_=ones16[:], compare_op=ALU.is_ge, fill=0.0, base=0,
                                    pattern=[[1, P]], channel_multiplier=-1).then_inc(consts, 1)
            for buf, pattern, rows in ((iota16, [[1, P]], 0), (iota_e, [[1, L0.E]], 0), (thr, [[P, NT]], 0),
                                       (tokid, [[P, NT]], 1)):
                nc.gpsimd.iota(buf[:], pattern, base=0, channel_multiplier=rows,
                               allow_small_or_imprecise_dtypes=True).then_inc(consts, 1)

            pool.wait_ge(c_mag, 1)
            link(nc.gpsimd.tensor_tensor(v_c, v_c, c_c, ALU.add))
            nc.gpsimd.tensor_tensor(wq.rearrange("p b k n -> p (b k n)"), v_c, c_c, ALU.subtract).then_inc(wq_ready, 1)

            def shared_pass(L, i):
                q = M[L.name]["pass"][i]
                for t in range(NT + 1):
                    if t < NT:
                        pool.wait_ge(q["evacuated"], t + 1)
                        if t >= 2:
                            pool.wait_ge(q["ht_done"], t - 1)
                        nc.gpsimd.tensor_tensor(hh[:, t % 2, 0:2 * L.J], sg[:, t % 2, 0:2 * L.J], up[:, t % 2, 0:2 * L.J],
                                                ALU.mult).then_inc(q["h_ready"], 1)
                    if t >= 1:
                        pool.wait_ge(q["y_copied"], t)
                        nc.gpsimd.tensor_tensor(x_sb[:, t - 1, :], x_sb[:, t - 1, :], ysb[:, (t - 1) % 2, :],
                                                ALU.add).then_inc(q["added"], 1)

            def gathers(L):
                m, d = M[L.name], small[L.name]
                pool.wait_ge(m["xn_stored"], 16)
                pool.wait_ge(m["table"], 1)

                def turn(base, group, first, last):
                    for j in range(UNROLL):
                        s = base + j
                        if not first:
                            pool.wait_ge(m["t_done"], s - UNROLL + 1)
                        nc.gpsimd.tensor_copy(gidx[:, j:j + 1], d["tab"][:, bass.ds(s, 1)]).then_inc(m["idx_col"], 1)
                        pool.wait_ge(m["idx_col"], s + 1)
                        pool.sem_inc(m["idx_seen"], 1)
                        nc.gpsimd.indirect_dma_start(
                            out=xg[:, j, :], out_offset=None, in_=xn_d[L.name],
                            in_offset=bass.IndirectOffsetOnAxis(ap=gidx[:, j:j + 1], axis=0)).then_inc(m["xg_in"][j], 16)

                turns(pool, L, turn)

            def gather_back(L):
                m, d = M[L.name], small[L.name]
                for j in range(UNROLL):
                    pool.wait_ge(m["y_stored"][j], 16 * (L.tiles // UNROLL))
                for t in range(NT):
                    for k in range(L.K):
                        nc.gpsimd.indirect_dma_start(
                            out=back_rows[L.name][:, t, k, :], out_offset=None, in_=ys_d[L.name],
                            in_offset=bass.IndirectOffsetOnAxis(ap=d["back"][:, t, k:k + 1], axis=0)
                        ).then_inc(m["rows_back"][t], 16)

            for L in (L0, L1):
                shared_pass(L, 0)
                gathers(L)
                gather_back(L)

        @block.scalar
        def _(act):
            act.dma_start(v_c.rearrange("p (b k n) -> p b k n", b=NB, k=C),
                          ctxT.rearrange("b (k p) n -> p b k n", p=P)).then_inc(ctxT_in, 16)
            act.dma_start(rw0[:], router_w0).then_inc(small_in, 16)
            act.dma_start(rb0[:], router_b0).then_inc(small_in, 16)
            act.dma_start(rw1[:], router_w1).then_inc(small_in, 16)
            act.dma_start(gamma_sb[:], gamma.to_broadcast([P, 1])).then_inc(small_in, 16)

            for i in range(2):
                act.wait_ge(xqT_done, i + 1)
                nc.scalar.activation(xqT[:, 4 * i:4 * i + 4].rearrange("p t k m -> p (t k m)"),
                                     bank[i][:].bitcast(BF16), ACT.Copy).then_inc(xqT_sb, 1)

            def router_copies(L):
                m = M[L.name]
                for t in range(NT):
                    act.wait_ge(m["rt_T"], t + 1)
                    nc.scalar.activation(RS[L.name]["xT"][:, t].rearrange("p c m -> p (c m)"), bank[t % 2][:, 0:H],
                                         ACT.Copy).then_inc(m["rt_Tsb"], 1)

            def shared_pass(L, i, alone):
                q, J2 = M[L.name]["pass"][i], 2 * L.J
                for t in range(NT + 1):
                    if t < NT:
                        act.wait_ge(q["g_done"], t + 1)
                        if t >= 2:
                            act.wait_ge(q["h_ready"], t - 1)
                        ins = nc.scalar.activation(sg[:, t % 2, 0:J2], bank[4 + t % 2][:, 0:J2], ACT.Silu)
                        if alone:
                            ins = nc.scalar.activation(up[:, t % 2, 0:J2], bank[4 + t % 2][:, J2:2 * J2], ACT.Copy)
                        ins.then_inc(q["evacuated"], 1)
                    if t >= 1:
                        act.wait_ge(q["ht_done"], t)
                        if t >= 3:
                            act.wait_ge(q["d_done"], t - 2)
                        nc.scalar.activation(hT[0:L.J, (t - 1) % 2].rearrange("p a m -> p (a m)"), bank[6][0:L.J, 0:2 * P],
                                             ACT.Copy).then_inc(q["hT_copied"], 1)
                        if alone:
                            act.wait_ge(q["d_done"], t)
                            if t >= 3:
                                act.wait_ge(q["added"], t - 2)
                            nc.scalar.activation(ysb[:, (t - 1) % 2, :], bank[7][:, 0:H], ACT.Copy).then_inc(q["y_copied"], 1)

            def tiles(L):
                m = M[L.name]

                def xT_copy(s, j, early):
                    act.wait_ge(m["t_done"], s + 1)
                    if not early:
                        act.wait_ge(m["g_done"], s - 1)
                    nc.scalar.activation(xT[:, j % 2].rearrange("p c m -> p (c m)"), bank[j % 2][:, 0:H],
                                         ACT.Copy).then_inc(m["xT_copied"], 1)

                def turn(base, group, first, last):
                    if first:
                        xT_copy(0, 0, True)
                    for j in range(UNROLL):
                        s = base + j
                        if not (last and j == UNROLL - 1):
                            xT_copy(s + 1, j + 1, first and j + 1 < 2)
                        act.wait_ge(m["g_done"], s + 1)
                        if not first or j >= 2:
                            act.wait_ge(m["h_ready"], s - 1)
                        nc.scalar.activation(sg[:, j % 2, 0:2 * L.J], bank[2 + j % 2][:, 0:2 * L.J],
                                             ACT.Silu).then_inc(m["sg_ready"], 1)

                turns(act, L, turn)

            router_copies(L0)
            shared_pass(L0, 0, True)
            tiles(L0)

            act.wait_ge(M["m0"]["exp_in"], 1)
            nc.scalar.activation(small["m0"]["rw"][:], small["m0"]["rw"][:], ACT.Exp).then_inc(M["m0"]["exp_out"], 1)

            def softmax_exp(g):
                act.wait_ge(nm_ready, g + 1)
                if g >= 3:
                    act.wait_ge(tp_done, g - 2)
                for q in range(2):
                    nc.scalar.activation(pr_sb[:, g % 3, q, :], bank[g % 3][:, q * H:(q + 1) * H], ACT.Exp,
                                         bias=small["nm"][:, g % 3, q:q + 1],
                                         accum_out=small["rsum"][:, g % 3, q:q + 1]).then_inc(p_raw, 1)

            def pT_copy(g):
                act.wait_ge(tp_done, g + 1)
                if g >= 2:
                    act.wait_ge(av_done, g - 1)
                nc.scalar.activation(pT_sb[:, g % 2].rearrange("p k q -> p (k q)"), bank[3 + g % 2][:],
                                     ACT.Copy).then_inc(pT_ready, 1)

            softmax_exp(0)
            softmax_exp(1)
            for g in range(nheads):
                pT_copy(g)
                if g + 2 < nheads:
                    softmax_exp(g + 2)
            router_copies(L1)
            act.wait_ge(M["m1"]["exp_in"], 1)
            nc.scalar.activation(small["m1"]["lg"][:], small["m1"]["lg"][:], ACT.Exp).then_inc(M["m1"]["exp_out"], 1)
            shared_pass(L1, 0, True)
            tiles(L1)
            shared_pass(L1, 1, False)

        @block.vector
        def _(dve):
            step = [0]

            def link(ins):
                step[0] += 1
                ins.then_inc(dve_step, 1)
                dve.wait_ge(dve_step, step[0])

            V = nc.vector

            def layernorm(tiles, dst_ready=None, scale=1.0, arrived=None):
                a, b = tiles[0], tiles[-1] + 1
                for t in tiles:
                    if arrived is not None and t % 2 == 0:
                        dve.wait_ge(arrived[t // 2], 16)
                    ins = V.bn_stats(st[:, t, :], x_sb[:, t, :])
                link(ins)
                for t in tiles:
                    ins = V.bn_aggr(mv[:, t, :], st[:, t, :])
                link(ins)
                v, r, w = ve[:, a:b], rstd[:, a:b], nt[:, a:b]
                link(V.tensor_scalar(v, mv[:, a:b, 1], LN_EPS, None, ALU.add))
                link(V.tensor_scalar(r.bitcast(I32), v.bitcast(I32), -0.5, float(0x5F3759DF), ALU.mult, ALU.add))
                for _ in range(3):
                    link(V.tensor_tensor(w, v, r, ALU.mult))
                    link(V.scalar_tensor_tensor(out=w, in0=w, scalar=-0.5, in1=r, op0=ALU.mult, op1=ALU.mult))
                    link(V.scalar_tensor_tensor(out=r, in0=w, scalar=1.5, in1=r, op0=ALU.add, op1=ALU.mult))
                if scale != 1.0:
                    link(V.tensor_scalar(r, r, scale, None, ALU.mult))
                for t in tiles:
                    ins = V.tensor_scalar(xn[:, t, :], x_sb[:, t, :], mv[:, t, 0:1], rstd[:, t:t + 1],
                                          ALU.subtract, ALU.mult)
                    if dst_ready is not None:
                        ins.then_inc(dst_ready, 1)
                return ins

            def power_of_two(c, v):
                link(V.tensor_scalar(c.bitcast(I32), v.bitcast(I32), 0x7F800000, None, ALU.bitwise_and))
                return V.tensor_scalar(c, c, 2.0 ** -6, 1.5 * 2.0 ** 20, ALU.max, ALU.mult)

            dve.wait_ge(ctxT_in, 16)
            ctx16 = v_c.rearrange("p (a n) -> p a n", n=P)
            V.tensor_reduce(amc[:], ctx16, AX.X, ALU.max, apply_absolute_value=True).then_inc(amc_ready, 1)
            dve.wait_ge(consts, 8)
            dve.wait_ge(amcT_done, 1)
            link(V.tensor_reduce(col16[0:16, :], bank[2][0:16, 0:P], AX.X, ALU.max))
            V.tensor_scalar(diag[0:16, :], ident[0:16, 0:16], col16[0:16, :], None, ALU.mult).then_inc(diag_ready, 1)
            dve.wait_ge(amb_done, 1)
            link(V.tensor_scalar(safe_c[:], bank[3][:, 0:16], W_EPS, None, ALU.max))
            link(V.reciprocal(rin_c[:], safe_c[:]))
            link(V.tensor_scalar(rin_c[:], rin_c[:], FP8_MAX, None, ALU.mult))
            link(V.tensor_tensor(ctx16, ctx16, rin_c[:].unsqueeze(2).broadcast_to([P, 16, P]), ALU.mult))
            power_of_two(c_c, v_c).then_inc(c_mag, 1)
            link(layernorm(range(NT), arrived=x_in))
            xn16 = v_x.rearrange("p (a n) -> p a n", n=P)
            link(V.tensor_reduce(amx[:], xn16, AX.X, ALU.max, apply_absolute_value=True))
            link(V.tensor_scalar(amx[:], amx[:], ACT_EPS, None, ALU.max))
            link(V.reciprocal(rin_x[:], amx[:]))
            link(V.tensor_scalar(rin_x[:], rin_x[:], FP8_MAX, None, ALU.mult))
            link(V.tensor_scalar(safe_c[:], safe_c[:], 1.0 / FP8_MAX, 1.0 / FP8_MAX, ALU.mult, ALU.mult))
            for t in range(NT):
                b = t // 2
                V.tensor_tensor(dq[:, t], amx[:, C * t:C * t + C].unsqueeze(2).broadcast_to([P, C, C]),
                                safe_c[:, 4 * b:4 * b + 4].rearrange("p (k n) -> p k n", k=C), ALU.mult)
            n = NT * H // 2
            for i in range(2):
                v, c = v_x[:, i * n:(i + 1) * n], c_x[:, i * n:(i + 1) * n]
                v16 = v.rearrange("p (a n) -> p a n", n=P)
                link(V.tensor_tensor(v16, v16, rin_x[:, 8 * i:8 * i + 8].unsqueeze(2).broadcast_to([P, 8, P]), ALU.mult))
                link(power_of_two(c, v))
                link(V.tensor_tensor(v, v, c, ALU.add))
                V.tensor_tensor(qx[:, i * n:(i + 1) * n], v, c, ALU.subtract).then_inc(xq_ready, 1)
            for t in range(NT):
                dve.wait_ge(xp_done, t + 1)
                for k in range(C):
                    for n in range(C):
                        ins = V.scalar_tensor_tensor(
                            out=x_sb[:, t, n * P:(n + 1) * P], in0=bank[4 + t % 2][:, k * H + n * P:k * H + (n + 1) * P],
                            scalar=dq[:, t, k, n:n + 1], in1=x_sb[:, t, n * P:(n + 1) * P], op0=ALU.mult, op1=ALU.add)
                        if n == C - 1 and k < C - 1:
                            link(ins)
                ins.then_inc(x1_ready, 1)
            dve.wait_ge(x1_ready, NT)

            def routing(L):
                m, d, r = M[L.name], small[L.name], RS[L.name]
                E, K = L.E, L.K
                dve.wait_ge(m["logits"], NT)
                link(V.tensor_copy(d["lg"][:], bank[2][:, 0:NT * E].rearrange("p (t e) -> p t e", t=NT)))
                if L is L1:
                    link(V.tensor_reduce(d["s1"][:], d["lg"][:], AX.X, ALU.max))
                    V.tensor_tensor(d["lg"][:], d["lg"][:], d["s1"][:].unsqueeze(2).broadcast_to([P, NT, E]),
                                    ALU.subtract).then_inc(m["exp_in"], 1)
                    dve.wait_ge(m["exp_out"], 1)
                    link(V.tensor_reduce(d["s2"][:], d["lg"][:], AX.X, ALU.add))
                    link(V.reciprocal(d["s2"][:], d["s2"][:]))
                    link(V.tensor_tensor(d["lg"][:], d["lg"][:], d["s2"][:].unsqueeze(2).broadcast_to([P, NT, E]),
                                         ALU.mult))
                for t in range(NT):
                    ins = V.max(d["top"][:, t, :], d["lg"][:, t, :])
                link(ins)
                for t in range(NT):
                    ins = V.max_index(d["idx"][:, t, :], d["top"][:, t, :], d["lg"][:, t, :])
                link(ins)
                link(V.tensor_copy(d["idxf"][:], d["idx"][:]))
                link(V.tensor_tensor(r["oh"], iota_e[:, 0:E].unsqueeze(1).unsqueeze(1).broadcast_to([P, NT, K, E]),
                                     d["idxf"][:, :, 0:K].unsqueeze(3).broadcast_to([P, NT, K, E]), ALU.is_equal))
                with nc.allow_low_precision(reason="sums of at most one 1"):
                    V.tensor_reduce(d["m16"][:], r["oh"].rearrange("p t k e -> p t e k"), AX.X,
                                    ALU.add).then_inc(m["mask"], 1)
                if L is L0:
                    V.tensor_tensor(d["rw"][:], d["top"][:, :, 0:K], d["top"][:, :, 0:1].broadcast_to([P, NT, K]),
                                    ALU.subtract).then_inc(m["exp_in"], 1)
                else:
                    V.tensor_copy(d["rw"][:], d["top"][:, :, 0:K])
                dve.wait_ge(m["counts"], 1)
                link(V.tensor_copy(d["cnt"][0:E, :], bank[3][0:E, 0:1]))
                link(V.tensor_scalar(d["junk"][0:E, :], thr[0:E, :], d["cnt"][0:E, :], None, ALU.is_lt, ALU.add,
                                     accum_out=d["ntc"][0:E, :]))
                V.tensor_scalar(d["ntr"][0:E, :], ones16[0:E, :], d["ntc"][0:E, :], None, ALU.mult).then_inc(m["ntiles"], 1)
                dve.wait_ge(m["starts"], 1)
                link(V.tensor_copy(d["endc"][0:E, :], bank[3][0:E, 8:9]))
                V.tensor_scalar(d["cmp"][0:E, :], iota16[0:E, 0:L.tiles], d["endc"][0:E, :], None,
                                ALU.is_ge).then_inc(m["cmp"], 1)
                link(V.tensor_scalar(d["startb"][:], bank[3][:, 16:16 + E], float(P), None, ALU.mult))
                link(V.tensor_tensor(r["base"], bank[2][:, 0:NT * E].rearrange("p (t e) -> p t e", t=NT),
                                     d["startb"][:].unsqueeze(1).broadcast_to([P, NT, E]), ALU.add))
                link(V.tensor_tensor(r["pr"], r["oh"], r["base"].unsqueeze(2).broadcast_to([P, NT, K, E]), ALU.mult))
                link(V.tensor_reduce(d["slotf"][:], r["pr"], AX.X, ALU.add))
                V.tensor_copy(d["back"][:], d["slotf"][:])
                link(V.tensor_copy(d["sloti"][:], d["slotf"][:]))
                V.tensor_scalar(d["ti"][:], d["sloti"][:], 7, None, ALU.logical_shift_right)
                link(V.tensor_scalar(d["pi"][:], d["sloti"][:], P - 1, None, ALU.bitwise_and))
                V.tensor_copy(d["tf"][:], d["ti"][:])
                link(V.tensor_copy(d["pf"][:], d["pi"][:]))
                for t in range(NT):
                    for k in range(K):
                        V.tensor_scalar(r["pos1"][:, t * K + k, :], iota16[:], d["pf"][:, t, k:k + 1], None, ALU.is_equal)
                        V.tensor_scalar(r["til1"][:, t * K + k, :], iota16[:, 0:L.tiles], d["tf"][:, t, k:k + 1],
                                        tokid[:, t:t + 1], ALU.is_equal, ALU.mult).then_inc(m["onehots"], 1)
                dve.wait_ge(m["owner"], 1)
                link(V.tensor_scalar(d["te"][:], bank[1][0:1, 0:L.tiles], float(E - 1), None, ALU.min))
                V.tensor_scalar(d["etab"][:], d["te"][:], float(L.S), float(L.stride), ALU.add,
                                ALU.mult).then_inc(m["table_e"], 1)
                dve.wait_ge(m["tokens"], 1)
                V.tensor_copy(d["tab"][:], bank[0][:, 0:L.tiles]).then_inc(m["table"], 1)

            def tiles(L):
                m = M[L.name]
                J2 = 2 * L.J

                def ht_copy(s, j, early):
                    dve.wait_ge(m["ht_done"], s + 1)
                    if not early:
                        dve.wait_ge(m["d_done"], s - 1)
                    V.tensor_copy(hT[0:L.J, j % 2].rearrange("p a m -> p (a m)"),
                                  bank[4 + j % 2][0:L.J, 0:2 * P]).then_inc(m["hT_copied"], 1)

                def y_copy(s, j, stores):
                    dve.wait_ge(m["d_done"], s + 1)
                    if stores is not None:
                        dve.wait_ge(m["y_stored"][j % UNROLL], 16 * stores)
                    V.tensor_copy(ysb[:, j % UNROLL, :], bank[6 + j % 2][:, 0:H]).then_inc(m["y_copied"], 1)

                def turn(base, group, first, last):
                    for j in range(UNROLL):
                        s = base + j
                        if not (first and j == 0):
                            ht_copy(s - 1, j - 1, first and j - 1 < 2)
                        dve.wait_ge(m["sg_ready"], s + 1)
                        if not first or j >= 2:
                            dve.wait_ge(m["ht_done"], s - 1)
                        V.tensor_tensor(hh[:, j % 2, 0:J2], sg[:, j % 2, 0:J2], bank[2 + j % 2][:, J2:2 * J2],
                                        ALU.mult).then_inc(m["h_ready"], 1)
                        if j >= 1:
                            y_copy(s - 1, j - 1, None if first else group)
                        elif not first:
                            y_copy(s - 1, j - 1, None if isinstance(group, int) and group == 1 else group - 1)
                    if last:
                        ht_copy(base + UNROLL - 1, UNROLL - 1, False)
                        y_copy(base + UNROLL - 1, UNROLL - 1, group)

                turns(dve, L, turn, early=2)

            def combine(L, t, ready):
                m, d, rows = M[L.name], small[L.name], back_rows[L.name]
                dve.wait_ge(m["rows_back"][t], 16 * L.K)
                for k in range(L.K):
                    ins = V.scalar_tensor_tensor(out=x_sb[:, t, :], in0=rows[:, t, k, :], scalar=d["rw"][:, t, k:k + 1],
                                                 in1=x_sb[:, t, :], op0=ALU.mult, op1=ALU.add)
                    if k < L.K - 1:
                        link(ins)
                ins.then_inc(ready, 1)

            layernorm(range(NT), M["m0"]["xn_ready"])
            routing(L0)
            tiles(L0)
            d = small["m0"]
            dve.wait_ge(M["m0"]["exp_out"], 1)
            link(V.tensor_reduce(d["s2"][:], d["rw"][:], AX.X, ALU.add))
            link(V.reciprocal(d["s2"][:], d["s2"][:]))
            link(V.tensor_scalar(d["s2"][:], d["s2"][:], ROUTED_SCALE, None, ALU.mult))
            link(V.tensor_tensor(d["rw"][:], d["rw"][:], d["s2"][:].unsqueeze(2).broadcast_to([P, NT, L0.K]), ALU.mult))

            def head_max(g):
                dve.wait_ge(s_done, g + 1)
                if g >= 3:
                    dve.wait_ge(p_raw, 2 * g - 4)
                V.tensor_reduce(small["nm"][:, g % 3, :], bank[g % 3][:].rearrange("p (q k) -> p q k", q=2),
                                AX.X, ALU.max, negate=True).then_inc(nm_ready, 1)

            def head_norm(g):
                dve.wait_ge(p_raw, 2 * g + 2)
                link(V.reciprocal(small["rinv"][:, g % 3, :], small["rsum"][:, g % 3, :]))
                for q in range(2):
                    ins = V.tensor_scalar(pr_sb[:, g % 3, q, :], pr_sb[:, g % 3, q, :], small["rinv"][:, g % 3, q:q + 1],
                                          None, ALU.mult)
                ins.then_inc(p_ready, 1)

            def tile_out(t):
                dve.wait_ge(av_done, HPT * (t + 1))
                V.scalar_tensor_tensor(out=x_sb[:, t, :], in0=bank[5 + t % 2][:, 0:H], scalar=gamma_sb[:], in1=x_sb[:, t, :],
                                       op0=ALU.mult, op1=ALU.add).then_inc(x3_ready, 1)

            def take(t):
                combine(L0, t, x2_ready)
                dve.wait_ge(x2_ready, t + 1)

            dve.wait_ge(small_in, 64)
            dve.wait_ge(M["m0"]["pass"][0]["added"], NT)
            take(0)
            layernorm([0], q_ready, SCALE)
            between = {0: [lambda: take(1)], 1: [lambda: layernorm([1], q_ready, SCALE)]}
            for t in range(2, NT, 2):
                at = HPT * (t - 1) - 2 if t > 2 else HPT
                between.setdefault(at, []).append(lambda t=t: take(t))
                between.setdefault(at + 1, []).append(lambda t=t: take(t + 1))
                between.setdefault(at + 2 if t > 2 else at + 1, []).append(lambda t=t: layernorm([t, t + 1], q_ready, SCALE))
            head_max(0)
            head_max(1)
            head_norm(0)
            for g in range(nheads):
                for work in between.get(g - 1, []):
                    work()
                if g + 2 < nheads:
                    head_max(g + 2)
                if g + 1 < nheads:
                    head_norm(g + 1)
                if g % HPT == 1 and g > HPT:
                    tile_out(g // HPT - 1)
            tile_out(NT - 1)
            dve.wait_ge(x3_ready, NT)
            layernorm(range(NT), M["m1"]["xn_ready"])
            routing(L1)
            tiles(L1)

            q, J2 = M["m1"]["pass"][1], 2 * L1.J
            dve.wait_ge(M["m1"]["pass"][0]["added"], NT)
            for t in range(NT + 1):
                if t < NT:
                    dve.wait_ge(q["evacuated"], t + 1)
                    if t >= 2:
                        dve.wait_ge(q["ht_done"], t - 1)
                    V.tensor_tensor(hh[:, t % 2, 0:J2], sg[:, t % 2, 0:J2], bank[4 + t % 2][:, J2:2 * J2],
                                    ALU.mult).then_inc(q["h_ready"], 1)
                if t >= 1:
                    dve.wait_ge(q["d_done"], t)
                    V.tensor_tensor(x_sb[:, t - 1, :], x_sb[:, t - 1, :], bank[7][:, 0:H], ALU.add).then_inc(q["added"], 1)
            dve.wait_ge(q["added"], NT)
            for t in range(NT):
                combine(L1, t, out_ready)

        @block.tensor
        def _(pe):
            T = nc.tensor
            pe.wait_ge(consts, 8)
            pe.wait_ge(amc_ready, 1)
            T.transpose(bank[2][0:16, 0:P], amc[:], ident[:]).then_inc(amcT_done, 1)
            pe.wait_ge(diag_ready, 1)
            T.matmul(bank[3][:, 0:16], ones32[0:16, :], diag[0:16, :], start=True, stop=True).then_inc(amb_done, 1)
            for i in range(2):
                pe.wait_ge(xq_ready, i + 1)
                b16 = bank[i][:].bitcast(BF16)
                for a in range(8):
                    ins = T.transpose(b16[:, a * P:(a + 1) * P], qx[:, (8 * i + a) * P:(8 * i + a + 1) * P], ident16[:])
                ins.then_inc(xqT_done, 1)
                pe.wait_ge(wq_ready, 1)
                pe.wait_ge(xqT_sb, i + 1)
                for t in range(4 * i, 4 * i + 4):
                    if t >= 2:
                        pe.wait_ge(x1_ready, t - 1)
                    for k in range(C):
                        ins = T.matmul(bank[4 + t % 2][:, k * H:(k + 1) * H], xqT[:, t, k, :], wq[:, t // 2, k, :],
                                       start=True, stop=True)
                    ins.then_inc(xp_done, 1)

            class Pass:

                def __init__(self, L, i):
                    self.L, self.i, self.t = L, i, 0

                def steps(self, n):
                    L, q = self.L, M[self.L.name]["pass"][self.i]
                    J2, off = 2 * L.J, self.i * L.stride
                    for t in range(self.t, self.t + n):
                        if t < NT:
                            if t >= 2:
                                pe.wait_ge(q["evacuated"], t - 1)
                                pe.wait_ge(q["h_ready"], t - 1)
                            for c in range(C):
                                ins = T.matmul(bank[4 + t % 2][:, 0:2 * J2], RS[L.name]["xT"][:, t, c, :],
                                               arena[:, off + c * 2 * J2:off + (c + 1) * 2 * J2], start=(c == 0), stop=(c == C - 1))
                            ins.then_inc(q["g_done"], 1)
                        if t >= 1:
                            pe.wait_ge(q["h_ready"], t)
                            if t >= 2:
                                pe.wait_ge(q["hT_copied"], t - 1)
                            for a in range(2):
                                ins = T.transpose(bank[6][0:L.J, a * P:(a + 1) * P], hh[:, (t - 1) % 2, a * L.J:(a + 1) * L.J],
                                                  ident[:])
                            ins.then_inc(q["ht_done"], 1)
                            pe.wait_ge(q["hT_copied"], t)
                            if t >= 2:
                                pe.wait_ge(q["y_copied"] if self.i == 0 else q["added"], t - 1)
                            for a in range(2):
                                ins = T.matmul(bank[7][:, 0:H], hT[0:L.J, (t - 1) % 2, a, :],
                                               arena[0:L.J, off + L.gu + a * H:off + L.gu + (a + 1) * H],
                                               start=(a == 0), stop=(a == 1))
                            ins.then_inc(q["d_done"], 1)
                    self.t += n

            def routing(L, rw, rb, w_in):
                m, d, r = M[L.name], small[L.name], RS[L.name]
                E, K = L.E, L.K

                def turn_rows(t):
                    pe.wait_ge(m["xn_ready"], t + 1)
                    if t >= 2:
                        pe.wait_ge(m["rt_Tsb"], t - 1)
                    for c in range(C):
                        ins = T.transpose(bank[t % 2][:, c * P:(c + 1) * P], xn[:, t, c * P:(c + 1) * P], ident[:])
                    ins.then_inc(m["rt_T"], 1)

                turn_rows(0)
                for t in range(NT):
                    if t + 1 < NT:
                        turn_rows(t + 1)
                    pe.wait_ge(m["rt_Tsb"], t + 1)
                    o = bank[2][:, t * E:(t + 1) * E]
                    if rb is not None:
                        T.matmul(o, ones32[0:1, :], rb[:], start=True, stop=False)
                    for c in range(C):
                        ins = T.matmul(o, r["xT"][:, t, c, :], rw[:, c, :], start=(c == 0 and rb is None), stop=(c == C - 1))
                    ins.then_inc(m["logits"], 1)
                shared = Pass(L, 0)
                pe.wait_ge(*w_in)
                shared.steps(3)
                pe.wait_ge(m["mask"], 1)
                for t in range(NT):
                    ins = T.matmul(bank[3][0:E, 0:1], d["m16"][:, t, :], ones16[:, 0:1], start=(t == 0), stop=(t == NT - 1))
                ins.then_inc(m["counts"], 1)
                T.matmul(bank[2][:, 0:NT * E], tri16[:], d["m16"][:].rearrange("p t e -> p (t e)"), start=True, stop=False,
                         skip_group_check=True)
                for t in range(NT - 1):
                    n = NT - 1 - t
                    T.matmul(bank[2][:, (t + 1) * E:NT * E], ones16[:],
                             d["m16"][:, t:t + 1, :].broadcast_to([P, n, E]), start=False, stop=(t == NT - 2),
                             skip_group_check=True)
                pe.wait_ge(m["ntiles"], 1)
                T.matmul(bank[3][:, 16:16 + E], d["ntr"][0:E, :], tri16[0:E, 0:E], start=True, stop=True)
                T.matmul(bank[3][0:E, 8:9], tri_in16[0:E, 0:E], d["ntr"][0:E, 0:1], start=True, stop=True).then_inc(m["starts"], 1)
                pe.wait_ge(m["cmp"], 1)
                T.matmul(bank[1][0:1, 0:L.tiles], ones16[0:E, 0:1], d["cmp"][0:E, :], start=True,
                         stop=True).then_inc(m["owner"], 1)
                shared.steps(4)
                for a in range(NT * K):
                    pe.wait_ge(m["onehots"], a + 1)
                    ins = T.matmul(bank[0][:, 0:L.tiles], r["pos1"][:, a, :], r["til1"][:, a, :], start=(a == 0),
                                   stop=(a == NT * K - 1))
                ins.then_inc(m["tokens"], 1)
                shared.steps(2)

            def tiles(L):
                m, d = M[L.name], small[L.name]
                J2 = 2 * L.J
                top = (L.S + L.E - 1) * L.stride
                pe.wait_ge(m["table_e"], 1)

                def weights_of(s):
                    return pe.value_load(d["etab"][0:1, bass.ds(s, 1)], min_val=0, max_val=top)

                def turn_in(s, j, group, early):
                    pe.wait_ge(m["xg_in"][j % UNROLL], 16 * (group + 1))
                    if not early:
                        pe.wait_ge(m["xT_copied"], s - 1)
                    for c in range(C):
                        ins = T.transpose(bank[j % 2][:, c * P:(c + 1) * P], xg[:, j % UNROLL, c * P:(c + 1) * P], ident[:])
                    ins.then_inc(m["t_done"], 1)

                def gate_up(j, c, off):
                    return T.matmul(bank[2 + j % 2][:, 0:2 * J2], xT[:, j % 2, c, :],
                                    arena[:, bass.ds(off + c * 2 * J2, 2 * J2)], start=(c == 0), stop=(c == C - 1))

                def turn_h(s, j, early):
                    pe.wait_ge(m["h_ready"], s + 1)
                    if not early:
                        pe.wait_ge(m["hT_copied"], s - 1)
                    for a in range(2):
                        ins = T.transpose(bank[4 + j % 2][0:L.J, a * P:(a + 1) * P], hh[:, j % 2, a * L.J:(a + 1) * L.J],
                                          ident[:])
                    ins.then_inc(m["ht_done"], 1)

                def down(s, j, off, early):
                    pe.wait_ge(m["hT_copied"], s + 1)
                    if not early:
                        pe.wait_ge(m["y_copied"], s - 1)
                    for a in range(2):
                        ins = T.matmul(bank[6 + j % 2][:, 0:H], hT[0:L.J, j % 2, a, :],
                                       arena[0:L.J, bass.ds(off + L.gu + a * H, H)], start=(a == 0), stop=(a == 1))
                    ins.then_inc(m["d_done"], 1)

                def turn(base, group, first, last):
                    before = None if first else weights_of(base - 1)
                    off = weights_of(base)
                    for j in range(UNROLL):
                        s = base + j
                        early = first and j < 2
                        pe.wait_ge(m["xT_copied"], s + 1)
                        if not early:
                            pe.wait_ge(m["h_ready"], s - 1)
                        gate_up(j, 0, off)
                        if before is not None:
                            turn_h(s - 1, j - 1, first and j - 1 < 2)
                        if not (last and j == UNROLL - 1):
                            turn_in(s + 1, j + 1, group + (j + 1) // UNROLL, first and j + 1 < 2)
                        gate_up(j, 1, off).then_inc(m["g_done"], 1)
                        after = weights_of(s + 1) if j + 1 < UNROLL else None
                        if before is not None:
                            down(s - 1, j - 1, before, first and j - 1 < 2)
                        before, off = off, after
                    if last:
                        turn_h(base + UNROLL - 1, UNROLL - 1, False)
                        down(base + UNROLL - 1, UNROLL - 1, before, False)

                turn_in(0, 0, 0, True)
                turns(pe, L, turn)

            pe.wait_ge(small_in, 64)
            routing(L0, rw0, rb0, (w_shared, 32))
            pe.wait_ge(w_early, 32 * -(-(L0.E - LATE) // EARLY))
            pe.wait_ge(w_late, 32)
            tiles(L0)

            pe.wait_ge(k_in, 16)
            pe.wait_ge(v_in, 16)

            def scores(g):
                t, r0 = g // HPT, (g % HPT) * HEAD
                pe.wait_ge(q_ready, t + 1)
                if g >= 3:
                    pe.wait_ge(p_raw, 2 * g - 4)
                for q in range(2):
                    ins = T.matmul(bank[g % 3][:, q * H:(q + 1) * H], xn[r0:r0 + HEAD, t, q * P:(q + 1) * P],
                                   k_sb[r0:r0 + HEAD, t, :], start=True, stop=True)
                ins.then_inc(s_done, 1)

            def turn_p(g):
                pe.wait_ge(p_ready, g + 1)
                if g >= 2:
                    pe.wait_ge(pT_ready, g - 1)
                for k in range(2):
                    for q in range(2):
                        ins = T.transpose(bank[3 + g % 2][:, (2 * k + q) * P:(2 * k + q + 1) * P],
                                          pr_sb[:, g % 3, q, k * P:(k + 1) * P], ident[:])
                ins.then_inc(tp_done, 1)

            def values(g):
                t, r0 = g // HPT, (g % HPT) * HEAD
                pe.wait_ge(pT_ready, g + 1)
                if t >= 2:
                    pe.wait_ge(x3_ready, t - 1)
                for k in range(2):
                    row = (t % 2) * P + r0
                    ins = T.matmul(bank[5 + t % 2][r0:r0 + HEAD, 0:H], vT[:, t // 2, k, row:row + HEAD],
                                   pT_sb[:, g % 2, k, :], start=(k == 0), stop=(k == 1), tile_position=(0, r0))
                ins.then_inc(av_done, 1)

            scores(0)
            scores(1)
            for g in range(nheads + 1):
                if g + 2 < nheads:
                    scores(g + 2)
                if g < nheads:
                    turn_p(g)
                if g >= 1:
                    values(g - 1)
            routing(L1, rw1, None, (w1_in, 32))
            tiles(L1)
            Pass(L1, 1).steps(NT + 1)


def kernel(**inputs):
    import numpy as np
    import concourse.bacc as bacc
    from concourse.bass_utils import run_bass_kernel_spmd

    a = {k: np.asarray(v) for k, v in inputs.items()}

    def chunks(w):
        n, h = w.shape
        return np.ascontiguousarray(w.T.reshape(h // P, P, n).transpose(1, 0, 2))

    def experts(gate, up, down):
        e, i, h = gate.shape
        gu = np.concatenate([gate, up], axis=1).transpose(2, 0, 1).reshape(h // P, P, e, 2 * i).transpose(1, 2, 0, 3)
        dn = down.transpose(2, 0, 1).reshape(2, i // 2, e, h).transpose(1, 2, 0, 3)
        return np.ascontiguousarray(gu.reshape(P, e, -1)), np.ascontiguousarray(dn.reshape(i // 2, e, -1))

    def halves(w, i, axis):
        return np.stack(np.split(w, w.shape[axis] // i, axis=axis))

    i0 = a["L0_ffn_gate_w"].shape[1]
    gu0, dn0 = experts(*(np.concatenate([halves(a["L0_ffn_shared_" + n], i0, ax), a["L0_ffn_" + n]])
                         for n, ax in (("gate_w", 0), ("up_w", 0), ("down_w", 1))))
    i1 = a["L1_ffn_w1"].shape[1]
    gu1, dn1 = experts(*(np.concatenate([halves(a["L1_ffn_s" + n], i1, ax), a["L1_ffn_" + n]])
                         for n, ax in (("w1", 0), ("w2", 0), ("w3", 1))))
    x = a["x"]
    H = x.shape[2]
    arrays = {
        "x": x.reshape(-1, P, H), "ctx": a["ctx_2048"], "ctxT": np.ascontiguousarray(a["ctx_2048"].transpose(0, 2, 1)),
        "router_w0": chunks(a["L0_ffn_router_w"]), "router_b0": a["L0_ffn_router_b"].reshape(1, -1),
        "w_gu0": gu0, "w_dn0": dn0, "gamma": a["L1_xattn_gamma"].reshape(1, 1),
        "router_w1": chunks(a["L1_ffn_gate_w"]), "w_gu1": gu1, "w_dn1": dn1,
    }
    arrays = {k: np.ascontiguousarray(v) for k, v in arrays.items()}
    nc = bacc.Bacc("TRN2", target_bir_lowering=False, num_devices=1)
    args = [nc.dram_tensor(n, v.shape, mybir.dt.from_np(v.dtype), kind="ExternalInput").ap() for n, v in arrays.items()]
    out = nc.dram_tensor("out", arrays["x"].shape, F32, kind="ExternalOutput").ap()
    mk_xattn_ffn(nc, *args, out)
    r = run_bass_kernel_spmd(nc, [arrays], core_ids=[0])
    return r.results[0]["out"].reshape(x.shape)
```

```python
from contextlib import ExitStack

import numpy as np
import concourse.bass as bass
from concourse import mybir

ALU = mybir.AluOpType
ACT = mybir.ActivationFunctionType
AX = mybir.AxisListType
F32 = mybir.dt.float32
F16 = mybir.dt.float16
BF16 = mybir.dt.bfloat16
I32 = mybir.dt.int32
U32 = mybir.dt.uint32

P = 128
LN_EPS = 1e-5
FP8_MAX = 448.0
ACT_EPS = 1e-4
W_EPS = 1e-6
ROUTED_SCALE = 1.8
UNROLL = 8
BUFS = 4
EARLY = 9
HEAD = 32


class Moe:

    def __init__(self, name, E, K, half, shared, n_tok):
        self.name, self.E, self.K, self.J, self.S = name, E, K, half, shared
        most = (n_tok * K + (P - 1) * E) // P
        self.tiles = -(-most // UNROLL) * UNROLL
        self.gu = 2 * 2 * 2 * half


def mk_xattn_ffn(nc, x, ctx, ctxT, router_w0, router_b0, w_gu0, w_dn0, gamma, router_w1, w_gu1, w_dn1, out):
    NT, _, H = x.shape
    C = H // P
    n_tok = NT * P
    NB = ctx.shape[0]
    HPT = P // HEAD
    nheads = NT * HPT
    SCALE = float(HEAD) ** -0.5
    L0 = Moe("m0", router_w0.shape[2], 4, w_dn0.shape[0], 1, n_tok)
    L1 = Moe("m1", router_w1.shape[2], 2, w_dn1.shape[0], 2, n_tok)
    for L in (L0, L1):
        L.stride = L.gu + 2 * H

    with ExitStack() as es:
        def sb(name, shape, dt=F32):
            return es.enter_context(nc.sbuf_tensor(name, shape, dt))

        def sem(name):
            return es.enter_context(nc.semaphore(name))

        bank = [es.enter_context(nc.psum_tensor(f"bank{i}", [P, 512], F32)) for i in range(8)]

        W_COLS = (L0.S + L0.E) * L0.stride
        arena = sb("arena", [P, W_COLS])
        x_sb = sb("x_sb", [P, NT, H])
        xn = sb("xn", [P, NT, H])
        ident = sb("ident", [P, P])
        ident16 = sb("ident16", [P, P], BF16)
        tri16 = sb("tri16", [P, P], BF16)
        tri_in16 = sb("tri_in16", [P, P], BF16)
        ones16 = sb("ones16", [P, P], BF16)
        ones32 = sb("ones32", [P, P])
        iota16 = sb("iota16", [P, P], F16)
        iota_e = sb("iota_e", [P, L0.E])
        thr = sb("thr", [P, NT])
        tokid = sb("tokid", [P, NT])
        gamma_sb = sb("gamma_sb", [P, 1])
        rw0 = sb("rw0", [P, C, L0.E])
        rb0 = sb("rb0", [P, L0.E])
        rw1 = sb("rw1", [P, C, L1.E])
        xg = sb("xg", [P, BUFS, H])
        xT = sb("xT", [P, 2, C, P])
        sg = sb("sg", [P, 2, 2 * L0.J])
        up = sb("up", [P, 2, 2 * L0.J])
        hh = sb("hh", [P, 2, 2 * L0.J])
        hT = sb("hT", [P, 2, 2, P])
        ysb = sb("ysb", [P, BUFS, H])
        gidx = sb("gidx", [P, BUFS], U32)
        st = sb("st", [P, NT, 6])
        mv = sb("mv", [P, NT, 2])
        ve = sb("ve", [P, NT])
        nt = sb("nt", [P, NT])
        rstd = sb("rstd", [P, NT])
        amc = sb("amc", [P, 16])
        amx = sb("amx", [P, 16])
        col16 = sb("col16", [P, 1])
        diag = sb("diag", [P, 16])
        safe_c = sb("safe_c", [P, 16])
        rin_c = sb("rin_c", [P, 16])
        rin_x = sb("rin_x", [P, 16])
        dq = sb("dq", [P, NT, C, C])
        small = {L0.name: {}, L1.name: {}}

        def routed(name, shape_of, dt=F32, rows=P):
            flat = sb(name, [rows, max(int(np.prod(shape_of(L))) for L in (L0, L1))], dt)
            for L in (L0, L1):
                shape = shape_of(L)
                v = flat[:, 0:int(np.prod(shape))]
                small[L.name][name] = v.rearrange("p (t k) -> p t k", t=shape[0]) if len(shape) == 2 else v

        routed("lg", lambda L: (NT, L.E))
        routed("m16", lambda L: (NT, L.E), BF16)
        for n in ("top", "idxf"):
            routed(n, lambda L: (NT, 8))
        routed("idx", lambda L: (NT, 8), U32)
        for n, dt in (("rw", F32), ("slotf", F32), ("tf", F32), ("pf", F32), ("sloti", I32), ("ti", I32), ("pi", I32),
                      ("back", U32)):
            routed(n, lambda L: (NT, L.K), dt)
        for n in ("s1", "s2", "junk"):
            routed(n, lambda L: (NT,))
        for n in ("cnt", "ntc", "endc"):
            routed(n, lambda L: (1,))
        routed("ntr", lambda L: (P,), BF16)
        routed("cmp", lambda L: (L.tiles,), BF16)
        routed("startb", lambda L: (L.E,))
        routed("tab", lambda L: (L.tiles,), U32)
        routed("te", lambda L: (L.tiles,), rows=1)
        routed("etab", lambda L: (L.tiles,), I32, rows=1)
        for n in ("nm", "rsum", "rinv"):
            small[n] = sb("att_" + n, [P, 4, 2])

        def part(at, cols):
            return arena[:, at:at + cols], at + cols

        LATE = 4
        late0 = (W_COLS // L0.stride - LATE) * L0.stride
        at = late0
        v_c, at = part(at, NB * C * H)
        c_c, at = part(at, NB * C * H)
        c_x = c_c
        wq, at = part(at, NB * C * H // 2)
        assert at <= W_COLS
        wq = wq.bitcast(BF16).rearrange("p (b k n) -> p b k n", b=NB, k=C)
        v_x = xn[:].rearrange("p t h -> p (t h)")
        qx = ysb[:].rearrange("p s h -> p (s h)").bitcast(BF16)
        xqT = xg[:].rearrange("p s h -> p (s h)").bitcast(BF16).rearrange("p (t k m) -> p t k m", t=NT, k=C)
        RS = {}
        for L, at in ((L0, late0), (L1, 20000)):
            d = {}
            n = NT * L.K * L.E
            d["oh"], at0 = part(at, n)
            d["pr"], at0 = part(at0, n)
            d["base"], at0 = part(at0, NT * L.E)
            d["pos1"], at = part(at, NT * L.K * P // 2)
            d["til1"], at = part(at, NT * L.K * L.tiles // 2)
            at = max(at, at0)
            last = -(-(W_COLS - at) // L0.stride)
            d["xT"], at = part(at, NT * H)
            d["last"] = last
            d["xT"] = d["xT"].rearrange("p (t c m) -> p t c m", t=NT, c=C)
            d["oh"] = d["oh"].rearrange("p (t k e) -> p t k e", t=NT, k=L.K)
            d["pr"] = d["pr"].rearrange("p (t k e) -> p t k e", t=NT, k=L.K)
            d["base"] = d["base"].rearrange("p (t e) -> p t e", t=NT)
            d["pos1"] = d["pos1"].bitcast(F16).rearrange("p (a m) -> p a m", m=P)
            d["til1"] = d["til1"].bitcast(F16).rearrange("p (a m) -> p a m", m=L.tiles)
            assert at <= W_COLS
            RS[L.name] = d
        at = 0
        w1_all, at = part(at, (L1.S + L1.E) * L1.stride)
        vT, at = part(at, NB * C * H)
        vT = vT.rearrange("p (b k n) -> p b k n", b=NB, k=C)
        pr_sb, at = part(at, 4 * 2 * H)
        pT_sb, at = part(at, 2 * 2 * H)
        pr_sb = pr_sb.rearrange("p (b q k) -> p b q k", b=4, q=2)
        pT_sb = pT_sb.rearrange("p (b k q) -> p b k q", b=2, k=2)
        QK_PARTS = (((0, 0), (0, 2)), ((0, 2), (1, 0)), ((1, 1), (0, 2)), ((1, 2), (1, 1)))
        ks, at = part(at, 2 * nheads * H // 2)
        ks = ks.bitcast(BF16).rearrange("p (s g n) -> p s g n", s=2, g=nheads)
        qs, at = part(at, 2 * 2 * HPT * H // 2)
        qs = qs.bitcast(BF16).rearrange("p (b s g n) -> p b s g n", b=2, s=2, g=HPT)
        q3, at = part(at, 2 * 3 * H // 2)
        q3 = q3.bitcast(BF16).rearrange("p (b a n) -> p b a n", b=2, a=3)
        k_raw, at1 = part((L0.S + 2 * EARLY) * L0.stride, NT * H)
        k3, at1 = part(at1, 3 * NT * H // 2)
        k3 = k3.bitcast(BF16).rearrange("p (a m) -> p a m", a=3)
        assert at1 <= (L0.S + 3 * EARLY) * L0.stride
        assert at <= 30000
        back_rows = {}
        at = 30000
        for L in (L0, L1):
            r, _ = part(at, NT * L.K * H)
            back_rows[L.name] = r.rearrange("p (t k h) -> p t k h", t=NT, k=L.K)
            assert at + NT * L.K * H <= W_COLS

        xn_d = {L.name: nc.dram_tensor(L.name + "_xn", (n_tok, H), F32, kind="Internal").ap() for L in (L0, L1)}
        ys_d = {L.name: nc.dram_tensor(L.name + "_ys", (L.tiles * P, H), F32, kind="Internal").ap() for L in (L0, L1)}

        k3_d = nc.dram_tensor("k3_d", (3, n_tok, H), BF16, kind="Internal").ap()
        q3_d = nc.dram_tensor("q3_d", (3, n_tok, H), BF16, kind="Internal").ap()

        batch_in = [sem(f"batch_in{b}") for b in range(NB)]
        ctxT_in = sem("ctxT_in")
        k_raw_in, k3_ready, k3_stored = sem("k_raw_in"), sem("k3_ready"), sem("k3_stored")
        q3_ready, q3_stored, qs_in = sem("q3_ready"), sem("q3_stored"), [sem(f"qs_in{i}") for i in range(2)]
        small_in = sem("small_in")
        w_shared, w_early, w_late, w1_in = sem("w_shared"), sem("w_early"), sem("w_late"), sem("w1_in")
        consts = sem("consts")
        consts0 = sem("consts0")
        dve_step = sem("dve_step")
        pool_step = sem("pool_step")
        amc_ready, amcT_done, diag_ready, amb_done = (sem(n) for n in ("amc_ready", "amcT_done", "diag_ready", "amb_done"))
        c_mag, wq_ready, xq_ready, xqT_done, xqT_sb, xp_done, x1_ready = (
            sem(n) for n in ("c_mag", "wq_ready", "xq_ready", "xqT_done", "xqT_sb", "xp_done", "x1_ready"))

        rows_back = [sem(f"rows_back{t}") for t in range(NT)]
        rows_in = {L0.name: 16 * L0.K, L1.name: 16 * (L0.K + L1.K)}
        M = {}
        for L in (L0, L1):
            m = {n: sem(f"{L.name}_{n}") for n in (
                "xn_ready xn_stored rt_T rt_Tsb logits exp_in exp_out mask counts ntiles starts "
                "cmp owner table_e onehots tokens table idx_col idx_seen t_done xT_copied g_done "
                "sg_ready h_ready ht_done hT_copied d_done y_copied ").split()}
            m["xg_in"] = [sem(f"{L.name}_xg_in{i}") for i in range(BUFS)]
            m["y_stored"] = [sem(f"{L.name}_y_stored{i}") for i in range(BUFS)]
            m["early"] = {n: sem(f"{L.name}_early_{n}") for n in
                          "g_done evacuated h_ready ht_done hT_copied d_done y_copied added".split()}
            m["after"] = {n: sem(f"{L.name}_after_{n}") for n in
                          "g_done evacuated h_ready ht_done hT_copied d_done added".split()}
            M[L.name] = m
        x2_ready, s_done, nm_ready, p_raw, p_ready, tp_done, pT_ready, av_done, x3_ready = (
            sem(n) for n in ("x2_ready", "s_done", "nm_ready", "p_raw", "p_ready", "tp_done", "pT_ready", "av_done", "x3_ready"))
        rinv_ready, p1_ready, p2_ready = sem("rinv_ready"), sem("p1_ready"), sem("p2_ready")
        out_ready, stored = sem("out_ready"), sem("stored")

        block = es.enter_context(nc.Block())
        ALONE = 8

        def turns(eng, L, turn):
            n = L.tiles // UNROLL
            turn(0, 0, True, False)
            with eng.Fori(1, n - 1) as g:
                turn(g * UNROLL, g, False, False)
            turn((n - 1) * UNROLL, n - 1, False, True)

        every = {L.name: [(i, t) for i in range(L.S) for t in range(NT)] for L in (L0, L1)}
        n_early = {"m0": 6, "m1": 3}
        n_mid = {"m0": 2, "m1": 2}
        early_work = {n: every[n][:n_early[n]] for n in every}
        after_work = {n: every[n][n_early[n]:] for n in every}

        @block.sync
        def _(sp):
            for t in range(0, NT, 2):
                sp.dma_start(x_sb[:, t:t + 2, :], x[t:t + 2].rearrange("t p h -> p t h")).then_inc(batch_in[t // 2], 16)
            n0 = L0.S + L0.E

            def experts(L, a, b, w_gu, w_dn, done):
                w = arena[:, a * L.stride:b * L.stride].rearrange("p (e c) -> p e c", c=L.stride)
                sp.dma_start(w[:, :, 0:L.gu], w_gu[:, a:b, :]).then_inc(done, 16)
                sp.dma_start(w[0:L.J, :, L.gu:L.stride], w_dn[:, a:b, :]).then_inc(done, 16)

            def store_xn(L):
                m = M[L.name]
                sp.wait_ge(m["xn_ready"], NT)
                sp.dma_start(xn_d[L.name].rearrange("(t p) h -> p t h", p=P), xn[:]).then_inc(m["xn_stored"], 16)

            def store_tiles(L):
                m = M[L.name]

                def turn(base, group, first, last):
                    for j in range(UNROLL):
                        sp.wait_ge(m["y_copied"], base + j + 1)
                        b = j % BUFS
                        sp.dma_start(ys_d[L.name][bass.ds((base + j) * P, P), :], ysb[:, b, :]).then_inc(m["y_stored"][b], 16)

                turns(sp, L, turn)
                for b in range(BUFS):
                    sp.wait_ge(m["y_stored"][b], 16 * (L.tiles // BUFS))

            sp.wait_ge(ctxT_in, 16)
            experts(L0, 0, L0.S, w_gu0, w_dn0, w_shared)
            sp.dma_start(k_raw.rearrange("p (t n) -> p t n", t=NT), ctx.rearrange("b (k p) n -> p (b k) n", p=P)).then_inc(k_raw_in, 16)
            for i, a in enumerate(range(L0.S, n0 - LATE, EARLY)):
                if i == 2:
                    sp.wait_ge(k3_ready, 1)
                    for part_ in range(3):
                        sp.dma_start(k3_d[part_].rearrange("(t p) n -> p t n", p=P),
                                     k3[:, part_].rearrange("p (t n) -> p t n", t=NT)).then_inc(k3_stored, 16)
                    sp.wait_ge(k3_stored, 48)
                experts(L0, a, min(a + EARLY, n0 - LATE), w_gu0, w_dn0, w_early)
            store_xn(L0)
            last = RS["m0"]["last"]
            sp.wait_ge(M["m0"]["table"], 1)
            experts(L0, n0 - LATE, n0 - last, w_gu0, w_dn0, w_late)
            sp.wait_ge(M["m0"]["early"]["g_done"], n_early["m0"])
            sp.wait_ge(M["m0"]["after"]["g_done"], n_mid["m0"])
            experts(L0, n0 - last, n0, w_gu0, w_dn0, w_late)
            store_tiles(L0)
            sp.wait_ge(M["m0"]["d_done"], L0.tiles)
            def places(dst, src, g0, which, done):
                n = dst.shape[2]
                rows = src[:, g0 * HEAD:(g0 + n) * HEAD, :].rearrange("a (g r) n -> r a g n", r=HEAD)
                for i, parts in enumerate(QK_PARTS):
                    a, b = parts[which]
                    for s_, a_ in enumerate((a, b)):
                        sp.dma_start(dst[i * HEAD:(i + 1) * HEAD, s_], rows[:, a_]).then_inc(done, 16)

            def q_places(t):
                sp.wait_ge(q3_ready, t + 1)
                sp.dma_start(q3_d[:, t * P:(t + 1) * P, :].rearrange("a p n -> p a n"), q3[:, t % 2]).then_inc(q3_stored, 16)
                sp.wait_ge(q3_stored, 16 * (t + 1))
                if t >= 2:
                    sp.wait_ge(s_done, HPT * (t - 1))
                places(qs[:, t % 2], q3_d, t * HPT, 0, qs_in[t % 2])

            def kv(b):
                places(ks[:, :, 2 * b * HPT:2 * (b + 1) * HPT], k3_d, 2 * b * HPT, 1, batch_in[b])
                sp.dma_start(vT[:, b], ctxT[b].rearrange("(k p) n -> p k n", p=P)).then_inc(batch_in[b], 16)

            kv(0)
            q_places(0)
            q_places(1)
            kv(1)
            q_places(2)
            q_places(3)
            kv(2)
            kv(3)
            q_places(4)
            for t in range(NT):
                sp.wait_ge(rows_back[t], rows_in["m0"])
            cuts = [(L1.S + L1.E) * i // 3 for i in range(4)]
            for i in range(3):
                q_places(5 + i)
                experts(L1, cuts[i], cuts[i + 1], w_gu1, w_dn1, w1_in)
            store_xn(L1)
            store_tiles(L1)
            for t in range(NT):
                sp.wait_ge(out_ready, t + 1)
                sp.dma_start(out[t], x_sb[:, t, :]).then_inc(stored, 16)
            sp.wait_ge(stored, 16 * NT)

        @block.gpsimd
        def _(pool):
            step = [0]

            def link(ins):
                step[0] += 1
                ins.then_inc(pool_step, 1)
                pool.wait_ge(pool_step, step[0])

            nc.gpsimd.memset(ident[:], 0.0).then_inc(consts0, 1)
            nc.gpsimd.memset(ident16[:], 0.0).then_inc(consts0, 1)
            nc.gpsimd.memset(ones16[:], 1.0).then_inc(consts0, 1)
            nc.gpsimd.memset(ones32[:], 1.0).then_inc(consts0, 1)
            pool.wait_ge(consts0, 4)
            for i in (ident, ident16):
                nc.gpsimd.affine_select(out=i[:], in_=i[:], compare_op=ALU.not_equal, fill=1.0, base=0,
                                        pattern=[[-1, P]], channel_multiplier=1).then_inc(consts, 1)
            nc.gpsimd.affine_select(out=tri16[:], in_=ones16[:], compare_op=ALU.is_gt, fill=0.0, base=0,
                                    pattern=[[1, P]], channel_multiplier=-1).then_inc(consts, 1)
            nc.gpsimd.affine_select(out=tri_in16[:], in_=ones16[:], compare_op=ALU.is_ge, fill=0.0, base=0,
                                    pattern=[[1, P]], channel_multiplier=-1).then_inc(consts, 1)
            for buf, pattern, rows in ((iota16, [[1, P]], 0), (iota_e, [[1, L0.E]], 0), (thr, [[P, NT]], 0),
                                       (tokid, [[P, NT]], 1)):
                nc.gpsimd.iota(buf[:], pattern, base=0, channel_multiplier=rows,
                               allow_small_or_imprecise_dtypes=True).then_inc(consts, 1)

            pool.wait_ge(c_mag, 1)
            link(nc.gpsimd.tensor_tensor(v_c, v_c, c_c, ALU.add))
            nc.gpsimd.tensor_tensor(wq.rearrange("p b k n -> p (b k n)"), v_c, c_c, ALU.subtract).then_inc(wq_ready, 1)

            pool.wait_ge(k_raw_in, 16)
            link(nc.gpsimd.tensor_copy(k3[:, 0], k_raw))
            link(nc.gpsimd.tensor_tensor(k_raw, k_raw, k3[:, 0], ALU.subtract))
            link(nc.gpsimd.tensor_copy(k3[:, 1], k_raw))
            nc.gpsimd.tensor_tensor(k3[:, 2], k_raw, k3[:, 1], ALU.subtract).then_inc(k3_ready, 1)

            def early_shared(L):
                q, work = M[L.name]["early"], early_work[L.name]
                for n in range(len(work) + 1):
                    if n < len(work):
                        pool.wait_ge(q["evacuated"], n + 1)
                        if n >= 2:
                            pool.wait_ge(q["ht_done"], n - 1)
                        nc.gpsimd.tensor_tensor(hh[:, n % 2, 0:2 * L.J], sg[:, n % 2, 0:2 * L.J], up[:, n % 2, 0:2 * L.J],
                                                ALU.mult).then_inc(q["h_ready"], 1)
                    if n >= 1:
                        t = work[n - 1][1]
                        pool.wait_ge(q["y_copied"], n)
                        nc.gpsimd.tensor_tensor(x_sb[:, t, :], x_sb[:, t, :], ysb[:, (n - 1) % 2, :],
                                                ALU.add).then_inc(q["added"], 1)

            def gathers(L):
                m, d = M[L.name], small[L.name]
                pool.wait_ge(m["xn_stored"], 16)
                pool.wait_ge(m["table"], 1)

                def turn(base, group, first, last):
                    for j in range(UNROLL):
                        s, b = base + j, j % BUFS
                        if not first or j >= BUFS:
                            pool.wait_ge(m["t_done"], s - BUFS + 1)
                        nc.gpsimd.tensor_copy(gidx[:, b:b + 1], d["tab"][:, bass.ds(s, 1)]).then_inc(m["idx_col"], 1)
                        pool.wait_ge(m["idx_col"], s + 1)
                        pool.sem_inc(m["idx_seen"], 1)
                        nc.gpsimd.indirect_dma_start(
                            out=xg[:, b, :], out_offset=None, in_=xn_d[L.name],
                            in_offset=bass.IndirectOffsetOnAxis(ap=gidx[:, b:b + 1], axis=0)).then_inc(m["xg_in"][b], 16)

                turns(pool, L, turn)

            def gather_back(L):
                m, d = M[L.name], small[L.name]
                for b in range(BUFS):
                    pool.wait_ge(m["y_stored"][b], 16 * (L.tiles // BUFS))
                for t in range(NT):
                    for k in range(L.K):
                        nc.gpsimd.indirect_dma_start(
                            out=back_rows[L.name][:, t, k, :], out_offset=None, in_=ys_d[L.name],
                            in_offset=bass.IndirectOffsetOnAxis(ap=d["back"][:, t, k:k + 1], axis=0)
                        ).then_inc(rows_back[t], 16)

            def head_norm(g):
                pool.wait_ge(rinv_ready, g + 1)
                nc.gpsimd.tensor_scalar(pr_sb[:, g % 4, 1, :], pr_sb[:, g % 4, 1, :], small["rinv"][:, g % 4, 1:2],
                                        None, ALU.mult).then_inc(p1_ready, 1)

            early_shared(L0)
            gathers(L0)
            gather_back(L0)
            for g in range(ALONE, nheads):
                head_norm(g)
            early_shared(L1)
            gathers(L1)
            gather_back(L1)

        @block.scalar
        def _(act):
            act.dma_start(v_c.rearrange("p (b k n) -> p b k n", b=NB, k=C),
                          ctxT.rearrange("b (k p) n -> p b k n", p=P)).then_inc(ctxT_in, 16)
            act.dma_start(rw0[:], router_w0).then_inc(small_in, 16)
            act.dma_start(rb0[:], router_b0.to_broadcast([P, L0.E])).then_inc(small_in, 16)
            act.dma_start(rw1[:], router_w1).then_inc(small_in, 16)
            act.dma_start(gamma_sb[:], gamma.to_broadcast([P, 1])).then_inc(small_in, 16)

            for i in range(2):
                act.wait_ge(xqT_done, i + 1)
                nc.scalar.activation(xqT[:, 4 * i:4 * i + 4].rearrange("p t k m -> p (t k m)"),
                                     bank[i][:].bitcast(BF16), ACT.Copy).then_inc(xqT_sb, 1)

            def router_copies(L):
                m = M[L.name]
                for i in range(NT // 2):
                    act.wait_ge(m["rt_T"], i + 1)
                    nc.scalar.activation(RS[L.name]["xT"][:, 2 * i:2 * i + 2].rearrange("p t c m -> p (t c m)"),
                                         bank[i % 2][:], ACT.Copy).then_inc(m["rt_Tsb"], 1)

            def hT_out(L, q, n):
                act.wait_ge(q["ht_done"], n + 1)
                if n >= 2:
                    act.wait_ge(q["d_done"], n - 1)
                nc.scalar.activation(hT[0:L.J, n % 2].rearrange("p a m -> p (a m)"), bank[6][0:L.J, 0:2 * P],
                                     ACT.Copy).then_inc(q["hT_copied"], 1)

            def early_shared(L):
                q, J2, N = M[L.name]["early"], 2 * L.J, len(early_work[L.name])
                for n in range(N + 1):
                    if n >= 1:
                        hT_out(L, q, n - 1)
                    if n < N:
                        act.wait_ge(q["g_done"], n + 1)
                        if n >= 2:
                            act.wait_ge(q["h_ready"], n - 1)
                        nc.scalar.activation(sg[:, n % 2, 0:J2], bank[4 + n % 2][:, 0:J2], ACT.Silu)
                        nc.scalar.activation(up[:, n % 2, 0:J2], bank[4 + n % 2][:, J2:2 * J2],
                                             ACT.Copy).then_inc(q["evacuated"], 1)
                    if n >= 1:
                        act.wait_ge(q["d_done"], n)
                        if n >= 3:
                            act.wait_ge(q["added"], n - 2)
                        nc.scalar.activation(ysb[:, (n - 1) % 2, :], bank[7][:, 0:H], ACT.Copy).then_inc(q["y_copied"], 1)

            def after_shared(L, a, b):
                q, J2 = M[L.name]["after"], 2 * L.J
                for n in range(a, b + 1):
                    if n > a:
                        hT_out(L, q, n - 1)
                    if n < b:
                        act.wait_ge(q["g_done"], n + 1)
                        if n >= 2:
                            act.wait_ge(q["h_ready"], n - 1)
                        nc.scalar.activation(sg[:, n % 2, 0:J2], bank[4 + n % 2][:, 0:J2],
                                             ACT.Silu).then_inc(q["evacuated"], 1)

            def tiles(L):
                m = M[L.name]

                def xT_copy(s, j, early):
                    act.wait_ge(m["t_done"], s + 1)
                    if not early:
                        act.wait_ge(m["g_done"], s - 1)
                    nc.scalar.activation(xT[:, j % 2].rearrange("p c m -> p (c m)"), bank[j % 2][:, 0:H],
                                         ACT.Copy).then_inc(m["xT_copied"], 1)

                def turn(base, group, first, last):
                    if first:
                        xT_copy(0, 0, True)
                    for j in range(UNROLL):
                        s = base + j
                        if not (last and j == UNROLL - 1):
                            xT_copy(s + 1, j + 1, first and j + 1 < 2)
                        act.wait_ge(m["g_done"], s + 1)
                        if not first or j >= 2:
                            act.wait_ge(m["h_ready"], s - 1)
                        nc.scalar.activation(sg[:, j % 2, 0:2 * L.J], bank[2 + j % 2][:, 0:2 * L.J],
                                             ACT.Silu).then_inc(m["sg_ready"], 1)

                turns(act, L, turn)

            router_copies(L0)
            early_shared(L0)
            after_shared(L0, 0, n_mid["m0"])
            tiles(L0)

            act.wait_ge(M["m0"]["exp_in"], 1)
            nc.scalar.activation(small["m0"]["rw"][:], small["m0"]["rw"][:], ACT.Exp).then_inc(M["m0"]["exp_out"], 1)

            def softmax_exp(g):
                act.wait_ge(nm_ready, g + 1)
                if g >= 4:
                    act.wait_ge(tp_done, g - 3)
                for q in range(2):
                    nc.scalar.activation(pr_sb[:, g % 4, q, :], bank[g % 4][:, q * H:(q + 1) * H], ACT.Exp,
                                         bias=small["nm"][:, g % 4, q:q + 1],
                                         accum_out=small["rsum"][:, g % 4, q:q + 1]).then_inc(p_raw, 1)

            def pT_copy(g):
                act.wait_ge(tp_done, g + 1)
                if g >= 2:
                    act.wait_ge(av_done, g - 1)
                nc.scalar.activation(pT_sb[:, g % 2].rearrange("p k q -> p (k q)"), bank[4 + g % 2][:],
                                     ACT.Copy).then_inc(pT_ready, 1)

            def divide(g):
                act.wait_ge(rinv_ready, g + 1)
                nc.scalar.activation(pr_sb[:, g % 4, 0, :], pr_sb[:, g % 4, 0, :], ACT.Copy,
                                     scale=small["rinv"][:, g % 4, 0:1]).then_inc(p_ready, 1)

            for g in range(3):
                softmax_exp(g)
            divide(0)
            divide(1)
            for g in range(nheads):
                pT_copy(g)
                if g + 2 < nheads:
                    divide(g + 2)
                if g + 3 < nheads:
                    softmax_exp(g + 3)
            router_copies(L1)
            act.wait_ge(M["m1"]["exp_in"], 1)
            nc.scalar.activation(small["m1"]["lg"][:], small["m1"]["lg"][:], ACT.Exp).then_inc(M["m1"]["exp_out"], 1)
            early_shared(L1)
            after_shared(L1, 0, n_mid["m1"])
            tiles(L1)
            after_shared(L1, n_mid["m1"], len(after_work["m1"]))

        @block.vector
        def _(dve):
            step = [0]

            def link(ins):
                step[0] += 1
                ins.then_inc(dve_step, 1)
                dve.wait_ge(dve_step, step[0])

            V = nc.vector

            def layernorm(tiles, dst_ready=None, scale=1.0, arrived=None):
                a, b = tiles[0], tiles[-1] + 1
                for t in tiles:
                    if arrived is not None and t % 2 == 0:
                        dve.wait_ge(arrived[t // 2], 16)
                    ins = V.bn_stats(st[:, t, :], x_sb[:, t, :])
                link(ins)
                for t in tiles:
                    ins = V.bn_aggr(mv[:, t, :], st[:, t, :])
                link(ins)
                h, r, w = ve[:, a:b], rstd[:, a:b], nt[:, a:b]
                link(V.tensor_scalar(h, mv[:, a:b, 1], LN_EPS, -0.5 / scale ** 2, ALU.add, ALU.mult))
                link(V.tensor_scalar(r.bitcast(I32), h.bitcast(I32), -0.5, float(0x5F3759DF - 2 ** 30 - 2 ** 22),
                                     ALU.mult, ALU.add))
                for _ in range(3):
                    link(V.tensor_tensor(w, h, r, ALU.mult))
                    link(V.tensor_tensor(w, w, r, ALU.mult))
                    link(V.scalar_tensor_tensor(out=r, in0=w, scalar=1.5, in1=r, op0=ALU.add, op1=ALU.mult))
                for t in tiles:
                    ins = V.tensor_scalar(xn[:, t, :], x_sb[:, t, :], mv[:, t, 0:1], rstd[:, t:t + 1],
                                          ALU.subtract, ALU.mult)
                    if dst_ready is not None:
                        ins.then_inc(dst_ready, 1)
                return ins

            def power_of_two(c, v):
                link(V.tensor_scalar(c.bitcast(I32), v.bitcast(I32), 0x7F800000, None, ALU.bitwise_and))
                return V.tensor_scalar(c, c, 2.0 ** -6, 1.5 * 2.0 ** 20, ALU.max, ALU.mult)

            dve.wait_ge(ctxT_in, 16)
            ctx16 = v_c.rearrange("p (a n) -> p a n", n=P)
            V.tensor_reduce(amc[:], ctx16, AX.X, ALU.max, apply_absolute_value=True).then_inc(amc_ready, 1)
            dve.wait_ge(consts, 8)
            dve.wait_ge(amcT_done, 1)
            link(V.tensor_reduce(col16[0:16, :], bank[2][0:16, 0:P], AX.X, ALU.max))
            V.tensor_scalar(diag[0:16, :], ident[0:16, 0:16], col16[0:16, :], None, ALU.mult).then_inc(diag_ready, 1)
            dve.wait_ge(amb_done, 1)
            link(V.tensor_scalar(safe_c[:], bank[3][:, 0:16], W_EPS, None, ALU.max))
            link(V.reciprocal(rin_c[:], safe_c[:]))
            link(V.tensor_scalar(rin_c[:], rin_c[:], FP8_MAX, None, ALU.mult))
            link(V.tensor_tensor(ctx16, ctx16, rin_c[:].unsqueeze(2).broadcast_to([P, 16, P]), ALU.mult))
            power_of_two(c_c, v_c).then_inc(c_mag, 1)
            link(layernorm(range(NT), arrived=batch_in))
            xn16 = v_x.rearrange("p (a n) -> p a n", n=P)
            link(V.tensor_reduce(amx[:], xn16, AX.X, ALU.max, apply_absolute_value=True))
            link(V.tensor_scalar(amx[:], amx[:], ACT_EPS, None, ALU.max))
            link(V.reciprocal(rin_x[:], amx[:]))
            link(V.tensor_scalar(rin_x[:], rin_x[:], FP8_MAX, None, ALU.mult))
            link(V.tensor_scalar(safe_c[:], safe_c[:], 1.0 / FP8_MAX, 1.0 / FP8_MAX, ALU.mult, ALU.mult))
            for t in range(NT):
                b = t // 2
                V.tensor_tensor(dq[:, t], amx[:, C * t:C * t + C].unsqueeze(2).broadcast_to([P, C, C]),
                                safe_c[:, 4 * b:4 * b + 4].rearrange("p (k n) -> p k n", k=C), ALU.mult)
            n = NT * H // 2
            dve.wait_ge(wq_ready, 1)
            for i in range(2):
                v, c = v_x[:, i * n:(i + 1) * n], c_x[:, i * n:(i + 1) * n]
                v16 = v.rearrange("p (a n) -> p a n", n=P)
                link(V.tensor_tensor(v16, v16, rin_x[:, 8 * i:8 * i + 8].unsqueeze(2).broadcast_to([P, 8, P]), ALU.mult))
                link(power_of_two(c, v))
                link(V.tensor_tensor(v, v, c, ALU.add))
                V.tensor_tensor(qx[:, i * n:(i + 1) * n], v, c, ALU.subtract).then_inc(xq_ready, 1)
            for t in range(NT):
                dve.wait_ge(xp_done, t + 1)
                for k in range(C):
                    for n in range(C):
                        ins = V.scalar_tensor_tensor(
                            out=x_sb[:, t, n * P:(n + 1) * P], in0=bank[4 + t % 2][:, k * H + n * P:k * H + (n + 1) * P],
                            scalar=dq[:, t, k, n:n + 1], in1=x_sb[:, t, n * P:(n + 1) * P], op0=ALU.mult, op1=ALU.add)
                        if n == C - 1 and k < C - 1:
                            link(ins)
                ins.then_inc(x1_ready, 1)
            dve.wait_ge(x1_ready, NT)

            def routing(L):
                m, d, r = M[L.name], small[L.name], RS[L.name]
                E, K = L.E, L.K
                dve.wait_ge(m["logits"], NT)
                lg = bank[2][:, 0:NT * E].rearrange("p (t e) -> p t e", t=NT)
                if L is L0:
                    dve.wait_ge(small_in, 64)
                    link(V.tensor_tensor(d["lg"][:], lg, rb0[:].unsqueeze(1).broadcast_to([P, NT, E]), ALU.add))
                else:
                    link(V.tensor_copy(d["lg"][:], lg))
                if L is L1:
                    link(V.tensor_reduce(d["s1"][:], d["lg"][:], AX.X, ALU.max))
                    V.tensor_tensor(d["lg"][:], d["lg"][:], d["s1"][:].unsqueeze(2).broadcast_to([P, NT, E]),
                                    ALU.subtract).then_inc(m["exp_in"], 1)
                    dve.wait_ge(m["exp_out"], 1)
                    link(V.tensor_reduce(d["s2"][:], d["lg"][:], AX.X, ALU.add))
                    link(V.reciprocal(d["s2"][:], d["s2"][:]))
                    link(V.tensor_tensor(d["lg"][:], d["lg"][:], d["s2"][:].unsqueeze(2).broadcast_to([P, NT, E]),
                                         ALU.mult))
                for t in range(NT):
                    ins = V.max(d["top"][:, t, :], d["lg"][:, t, :])
                link(ins)
                for t in range(NT):
                    ins = V.max_index(d["idx"][:, t, :], d["top"][:, t, :], d["lg"][:, t, :])
                link(ins)
                link(V.tensor_copy(d["idxf"][:], d["idx"][:]))
                link(V.tensor_tensor(r["oh"], iota_e[:, 0:E].unsqueeze(1).unsqueeze(1).broadcast_to([P, NT, K, E]),
                                     d["idxf"][:, :, 0:K].unsqueeze(3).broadcast_to([P, NT, K, E]), ALU.is_equal))
                with nc.allow_low_precision(reason="sums of at most one 1"):
                    V.tensor_reduce(d["m16"][:], r["oh"].rearrange("p t k e -> p t e k"), AX.X,
                                    ALU.add).then_inc(m["mask"], 1)
                if L is L0:
                    V.tensor_tensor(d["rw"][:], d["top"][:, :, 0:K], d["top"][:, :, 0:1].broadcast_to([P, NT, K]),
                                    ALU.subtract).then_inc(m["exp_in"], 1)
                else:
                    V.tensor_copy(d["rw"][:], d["top"][:, :, 0:K])
                dve.wait_ge(m["counts"], 1)
                link(V.tensor_copy(d["cnt"][0:E, :], bank[3][0:E, 0:1]))
                link(V.tensor_scalar(d["junk"][0:E, :], thr[0:E, :], d["cnt"][0:E, :], None, ALU.is_lt, ALU.add,
                                     accum_out=d["ntc"][0:E, :]))
                V.tensor_scalar(d["ntr"][0:E, :], ones16[0:E, :], d["ntc"][0:E, :], None, ALU.mult).then_inc(m["ntiles"], 1)
                dve.wait_ge(m["starts"], 1)
                link(V.tensor_copy(d["endc"][0:E, :], bank[3][0:E, 8:9]))
                V.tensor_scalar(d["cmp"][0:E, :], iota16[0:E, 0:L.tiles], d["endc"][0:E, :], None,
                                ALU.is_ge).then_inc(m["cmp"], 1)
                link(V.tensor_scalar(d["startb"][:], bank[3][:, 16:16 + E], float(P), None, ALU.mult))
                link(V.tensor_tensor(r["base"], bank[2][:, 0:NT * E].rearrange("p (t e) -> p t e", t=NT),
                                     d["startb"][:].unsqueeze(1).broadcast_to([P, NT, E]), ALU.add))
                link(V.tensor_tensor(r["pr"], r["oh"], r["base"].unsqueeze(2).broadcast_to([P, NT, K, E]), ALU.mult))
                link(V.tensor_reduce(d["slotf"][:], r["pr"], AX.X, ALU.add))
                V.tensor_copy(d["back"][:], d["slotf"][:])
                link(V.tensor_copy(d["sloti"][:], d["slotf"][:]))
                V.tensor_scalar(d["ti"][:], d["sloti"][:], 7, None, ALU.logical_shift_right)
                link(V.tensor_scalar(d["pi"][:], d["sloti"][:], P - 1, None, ALU.bitwise_and))
                V.tensor_copy(d["tf"][:], d["ti"][:])
                link(V.tensor_copy(d["pf"][:], d["pi"][:]))
                link(V.tensor_tensor(r["til1"], iota16[:, 0:L.tiles].unsqueeze(1).broadcast_to([P, NT * K, L.tiles]),
                                     d["tf"][:].rearrange("p t k -> p (t k)").unsqueeze(2).broadcast_to([P, NT * K, L.tiles]),
                                     ALU.is_equal))
                for t in range(NT):
                    w = r["til1"][:, t * K:(t + 1) * K, :]
                    V.tensor_scalar(w, w, tokid[:, t:t + 1], None, ALU.mult)
                    for k in range(K):
                        V.tensor_scalar(r["pos1"][:, t * K + k, :], iota16[:], d["pf"][:, t, k:k + 1], None,
                                        ALU.is_equal).then_inc(m["onehots"], 1)
                dve.wait_ge(m["owner"], 1)
                link(V.tensor_scalar(d["te"][:], bank[1][0:1, 0:L.tiles], float(E - 1), None, ALU.min))
                V.tensor_scalar(d["etab"][:], d["te"][:], float(L.S), float(L.stride), ALU.add,
                                ALU.mult).then_inc(m["table_e"], 1)
                dve.wait_ge(m["tokens"], 1)
                V.tensor_copy(d["tab"][:], bank[0][:, 0:L.tiles]).then_inc(m["table"], 1)

            def after_shared(L, a, b):
                q, J2, work = M[L.name]["after"], 2 * L.J, after_work[L.name]
                for n in range(a, b + 1):
                    if n < b:
                        dve.wait_ge(q["evacuated"], n + 1)
                        if n >= 2:
                            dve.wait_ge(q["ht_done"], n - 1)
                        V.tensor_tensor(hh[:, n % 2, 0:J2], sg[:, n % 2, 0:J2], bank[4 + n % 2][:, J2:2 * J2],
                                        ALU.mult).then_inc(q["h_ready"], 1)
                    if n > a:
                        t = work[n - 1][1]
                        dve.wait_ge(q["d_done"], n)
                        V.tensor_tensor(x_sb[:, t, :], x_sb[:, t, :], bank[7][:, 0:H], ALU.add).then_inc(q["added"], 1)

            def tiles(L):
                m = M[L.name]
                J2 = 2 * L.J

                def ht_copy(s, j, early):
                    dve.wait_ge(m["ht_done"], s + 1)
                    if not early:
                        dve.wait_ge(m["d_done"], s - 1)
                    V.tensor_copy(hT[0:L.J, j % 2].rearrange("p a m -> p (a m)"),
                                  bank[4 + j % 2][0:L.J, 0:2 * P]).then_inc(m["hT_copied"], 1)

                def y_copy(s, j, first, group):
                    dve.wait_ge(m["d_done"], s + 1)
                    if not first or j >= BUFS:
                        dve.wait_ge(m["y_stored"][j % BUFS], 16 * (group * (UNROLL // BUFS) + j // BUFS))
                    V.tensor_copy(ysb[:, j % BUFS, :], bank[6 + j % 2][:, 0:H]).then_inc(m["y_copied"], 1)

                def turn(base, group, first, last):
                    for j in range(UNROLL):
                        s = base + j
                        if not (first and j == 0):
                            ht_copy(s - 1, j - 1, first and j - 1 < 2)
                        dve.wait_ge(m["sg_ready"], s + 1)
                        if not first or j >= 2:
                            dve.wait_ge(m["ht_done"], s - 1)
                        V.tensor_tensor(hh[:, j % 2, 0:J2], sg[:, j % 2, 0:J2], bank[2 + j % 2][:, J2:2 * J2],
                                        ALU.mult).then_inc(m["h_ready"], 1)
                        if not (first and j == 0):
                            y_copy(s - 1, j - 1, first, group)
                    if last:
                        ht_copy(base + UNROLL - 1, UNROLL - 1, False)
                        y_copy(base + UNROLL - 1, UNROLL - 1, False, group)

                turns(dve, L, turn)

            def combine(L, t, ready):
                m, d, rows = M[L.name], small[L.name], back_rows[L.name]
                dve.wait_ge(rows_back[t], rows_in[L.name])
                for k in range(L.K):
                    ins = V.scalar_tensor_tensor(out=x_sb[:, t, :], in0=rows[:, t, k, :], scalar=d["rw"][:, t, k:k + 1],
                                                 in1=x_sb[:, t, :], op0=ALU.mult, op1=ALU.add)
                    if k < L.K - 1:
                        link(ins)
                ins.then_inc(ready, 1)

            layernorm(range(NT), M["m0"]["xn_ready"])
            routing(L0)
            after_shared(L0, 0, n_mid["m0"])
            tiles(L0)
            d = small["m0"]
            dve.wait_ge(M["m0"]["exp_out"], 1)
            link(V.tensor_reduce(d["s2"][:], d["rw"][:], AX.X, ALU.add))
            link(V.reciprocal(d["s2"][:], d["s2"][:]))
            link(V.tensor_scalar(d["s2"][:], d["s2"][:], ROUTED_SCALE, None, ALU.mult))
            link(V.tensor_tensor(d["rw"][:], d["rw"][:], d["s2"][:].unsqueeze(2).broadcast_to([P, NT, L0.K]), ALU.mult))

            def head_max(g):
                dve.wait_ge(s_done, g + 1)
                if g >= 4:
                    dve.wait_ge(p_raw, 2 * g - 6)
                V.tensor_reduce(small["nm"][:, g % 4, :], bank[g % 4][:].rearrange("p (q k) -> p q k", q=2),
                                AX.X, ALU.max, negate=True).then_inc(nm_ready, 1)

            def head_inverse(g):
                dve.wait_ge(p_raw, 2 * g + 2)
                if g >= 4:
                    dve.wait_ge(p_ready, g - 3)
                if g >= ALONE + 4:
                    dve.wait_ge(p1_ready, g - 3 - ALONE)
                V.reciprocal(small["rinv"][:, g % 4, :], small["rsum"][:, g % 4, :]).then_inc(rinv_ready, 1)
                dve.wait_ge(rinv_ready, g + 1)
                if g < ALONE:
                    V.tensor_scalar(pr_sb[:, g % 4, 1, :], pr_sb[:, g % 4, 1, :], small["rinv"][:, g % 4, 1:2],
                                    None, ALU.mult).then_inc(p2_ready, 1)

            def tile_out(t):
                dve.wait_ge(av_done, HPT * (t + 1))
                V.scalar_tensor_tensor(out=x_sb[:, t, :], in0=bank[6 + t % 2][:, 0:H], scalar=gamma_sb[:], in1=x_sb[:, t, :],
                                       op0=ALU.mult, op1=ALU.add).then_inc(x3_ready, 1)

            def take(t):
                combine(L0, t, x2_ready)
                dve.wait_ge(x2_ready, t + 1)

            dve.wait_ge(small_in, 64)
            dve.wait_ge(M["m0"]["early"]["added"], n_early["m0"])
            dve.wait_ge(M["m0"]["after"]["added"], n_mid["m0"])
            def queries(tiles):
                link(layernorm(tiles, None, SCALE))
                for t in tiles:
                    if t >= 2:
                        dve.wait_ge(q3_stored, 16 * (t - 1))
                    ins = V.tensor_copy(q3[:, t % 2, 0], xn[:, t, :])
                link(ins)
                for t in tiles:
                    ins = V.tensor_tensor(xn[:, t, :], xn[:, t, :], q3[:, t % 2, 0], ALU.subtract)
                link(ins)
                for t in tiles:
                    ins = V.tensor_copy(q3[:, t % 2, 1], xn[:, t, :])
                link(ins)
                for t in tiles:
                    V.tensor_tensor(q3[:, t % 2, 2], xn[:, t, :], q3[:, t % 2, 1], ALU.subtract).then_inc(q3_ready, 1)

            take(0)
            queries([0])
            take(1)
            queries([1])
            take(2)
            take(3)
            between = {0: [lambda: queries([2, 3])]}
            for t in range(4, NT, 2):
                before = HPT * t - 12
                between.setdefault(before - 2, []).append(lambda t=t: take(t))
                between.setdefault(before - 1, []).append(lambda t=t: take(t + 1))
                between.setdefault(before, []).append(lambda t=t: queries([t, t + 1]))
            for g in range(3):
                head_max(g)
            for g in range(2):
                head_inverse(g)
            for g in range(nheads):
                for work in between.get(g, []):
                    work()
                if g + 3 < nheads:
                    head_max(g + 3)
                if g + 2 < nheads:
                    head_inverse(g + 2)
                if g % HPT == 1 and g > HPT:
                    t = g // HPT - 1
                    tile_out(t)
                    if t % 2:
                        dve.wait_ge(x3_ready, t + 1)
                        layernorm([t - 1, t], M["m1"]["xn_ready"])
            tile_out(NT - 1)
            dve.wait_ge(x3_ready, NT)
            layernorm([NT - 2, NT - 1], M["m1"]["xn_ready"])
            routing(L1)
            after_shared(L1, 0, n_mid["m1"])
            tiles(L1)

            dve.wait_ge(M["m1"]["early"]["added"], n_early["m1"])
            after_shared(L1, n_mid["m1"], len(after_work["m1"]))
            dve.wait_ge(M["m1"]["after"]["added"], len(after_work["m1"]))
            for t in range(NT):
                combine(L1, t, out_ready)

        @block.tensor
        def _(pe):
            T = nc.tensor
            pe.wait_ge(consts, 8)
            pe.wait_ge(amc_ready, 1)
            T.transpose(bank[2][0:16, 0:P], amc[:], ident[:]).then_inc(amcT_done, 1)
            pe.wait_ge(diag_ready, 1)
            T.matmul(bank[3][:, 0:16], ones32[0:16, :], diag[0:16, :], start=True, stop=True).then_inc(amb_done, 1)
            for i in range(2):
                pe.wait_ge(xq_ready, i + 1)
                b16 = bank[i][:].bitcast(BF16)
                for a in range(8):
                    ins = T.transpose(b16[:, a * P:(a + 1) * P], qx[:, (8 * i + a) * P:(8 * i + a + 1) * P], ident16[:])
                ins.then_inc(xqT_done, 1)
                pe.wait_ge(wq_ready, 1)
                pe.wait_ge(xqT_sb, i + 1)
                for t in range(4 * i, 4 * i + 4):
                    if t >= 2:
                        pe.wait_ge(x1_ready, t - 1)
                    for k in range(C):
                        ins = T.matmul(bank[4 + t % 2][:, k * H:(k + 1) * H], xqT[:, t, k, :], wq[:, t // 2, k, :],
                                       start=True, stop=True)
                    ins.then_inc(xp_done, 1)

            def shared_steps(L, part, a, b, start, end):
                q = M[L.name][part]
                work = (early_work if part == "early" else after_work)[L.name]
                J2 = 2 * L.J
                for n in range(start, end):
                    if n > a:
                        pe.wait_ge(q["h_ready"], n)
                        if n >= 2:
                            pe.wait_ge(q["hT_copied"], n - 1)
                        for h in range(2):
                            ins = T.transpose(bank[6][0:L.J, h * P:(h + 1) * P], hh[:, (n - 1) % 2, h * L.J:(h + 1) * L.J],
                                              ident[:])
                        ins.then_inc(q["ht_done"], 1)
                    if n < b:
                        i, t = work[n]
                        if n >= 2:
                            pe.wait_ge(q["evacuated"], n - 1)
                            pe.wait_ge(q["h_ready"], n - 1)
                        for c in range(C):
                            at = i * L.stride + c * 2 * J2
                            ins = T.matmul(bank[4 + n % 2][:, 0:2 * J2], RS[L.name]["xT"][:, t, c, :],
                                           arena[:, at:at + 2 * J2], start=(c == 0), stop=(c == C - 1))
                        ins.then_inc(q["g_done"], 1)
                    if n > a:
                        pe.wait_ge(q["hT_copied"], n)
                        if n >= 2:
                            pe.wait_ge(q["y_copied" if part == "early" else "added"], n - 1)
                        elif part == "after":
                            pe.wait_ge(M[L.name]["early"]["y_copied"], n_early[L.name])
                        for h in range(2):
                            at = work[n - 1][0] * L.stride + L.gu + h * H
                            ins = T.matmul(bank[7][:, 0:H], hT[0:L.J, (n - 1) % 2, h, :], arena[0:L.J, at:at + H],
                                           start=(h == 0), stop=(h == 1))
                        ins.then_inc(q["d_done"], 1)

            def routing(L, rw, w_in):
                m, d, r = M[L.name], small[L.name], RS[L.name]
                E, K = L.E, L.K

                def turn_rows(i):
                    pe.wait_ge(m["xn_ready"], 2 * i + 2)
                    if i >= 2:
                        pe.wait_ge(m["rt_Tsb"], i - 1)
                    for t in (2 * i, 2 * i + 1):
                        for c in range(C):
                            at = ((t % 2) * C + c) * P
                            ins = T.transpose(bank[i % 2][:, at:at + P], xn[:, t, c * P:(c + 1) * P], ident[:])
                    ins.then_inc(m["rt_T"], 1)

                turn_rows(0)
                for i in range(NT // 2):
                    if i + 1 < NT // 2:
                        turn_rows(i + 1)
                    pe.wait_ge(m["rt_Tsb"], i + 1)
                    for t in (2 * i, 2 * i + 1):
                        o = bank[2][:, t * E:(t + 1) * E]
                        for c in range(C):
                            ins = T.matmul(o, r["xT"][:, t, c, :], rw[:, c, :], start=(c == 0), stop=(c == C - 1))
                        ins.then_inc(m["logits"], 1)
                N = n_early[L.name]
                pe.wait_ge(*w_in)
                shared_steps(L, "early", 0, N, 0, 1)
                pe.wait_ge(m["mask"], 1)
                for t in range(NT):
                    ins = T.matmul(bank[3][0:E, 0:1], d["m16"][:, t, :], ones16[:, 0:1], start=(t == 0), stop=(t == NT - 1))
                ins.then_inc(m["counts"], 1)
                T.matmul(bank[2][:, 0:NT * E], tri16[:], d["m16"][:].rearrange("p t e -> p (t e)"), start=True, stop=False,
                         skip_group_check=True)
                for t in range(NT - 1):
                    n = NT - 1 - t
                    T.matmul(bank[2][:, (t + 1) * E:NT * E], ones16[:],
                             d["m16"][:, t:t + 1, :].broadcast_to([P, n, E]), start=False, stop=(t == NT - 2),
                             skip_group_check=True)
                pe.wait_ge(m["ntiles"], 1)
                T.matmul(bank[3][:, 16:16 + E], d["ntr"][0:E, :], tri16[0:E, 0:E], start=True, stop=True)
                T.matmul(bank[3][0:E, 8:9], tri_in16[0:E, 0:E], d["ntr"][0:E, 0:1], start=True, stop=True).then_inc(m["starts"], 1)
                pe.wait_ge(m["cmp"], 1)
                T.matmul(bank[1][0:1, 0:L.tiles], ones16[0:E, 0:1], d["cmp"][0:E, :], start=True,
                         stop=True).then_inc(m["owner"], 1)
                shared_steps(L, "early", 0, N, 1, N + 1)
                for a in range(NT * K):
                    pe.wait_ge(m["onehots"], a + 1)
                    ins = T.matmul(bank[0][:, 0:L.tiles], r["pos1"][:, a, :], r["til1"][:, a, :], start=(a == 0),
                                   stop=(a == NT * K - 1))
                ins.then_inc(m["tokens"], 1)
                shared_steps(L, "after", 0, n_mid[L.name], 0, n_mid[L.name] + 1)

            def tiles(L):
                m, d = M[L.name], small[L.name]
                J2 = 2 * L.J
                top = (L.S + L.E - 1) * L.stride
                pe.wait_ge(m["table_e"], 1)

                def weights_of(s):
                    return pe.value_load(d["etab"][0:1, bass.ds(s, 1)], min_val=0, max_val=top)

                def turn_in(s, j, group, early):
                    pe.wait_ge(m["xg_in"][j % BUFS], 16 * (group * (UNROLL // BUFS) + j // BUFS + 1))
                    if not early:
                        pe.wait_ge(m["xT_copied"], s - 1)
                    for c in range(C):
                        ins = T.transpose(bank[j % 2][:, c * P:(c + 1) * P], xg[:, j % BUFS, c * P:(c + 1) * P], ident[:])
                    ins.then_inc(m["t_done"], 1)

                def gate_up(j, c, off):
                    return T.matmul(bank[2 + j % 2][:, 0:2 * J2], xT[:, j % 2, c, :],
                                    arena[:, bass.ds(off + c * 2 * J2, 2 * J2)], start=(c == 0), stop=(c == C - 1))

                def turn_h(s, j, early):
                    pe.wait_ge(m["h_ready"], s + 1)
                    if not early:
                        pe.wait_ge(m["hT_copied"], s - 1)
                    for a in range(2):
                        ins = T.transpose(bank[4 + j % 2][0:L.J, a * P:(a + 1) * P], hh[:, j % 2, a * L.J:(a + 1) * L.J],
                                          ident[:])
                    ins.then_inc(m["ht_done"], 1)

                def down(s, j, off, early):
                    pe.wait_ge(m["hT_copied"], s + 1)
                    if not early:
                        pe.wait_ge(m["y_copied"], s - 1)
                    for a in range(2):
                        ins = T.matmul(bank[6 + j % 2][:, 0:H], hT[0:L.J, j % 2, a, :],
                                       arena[0:L.J, bass.ds(off + L.gu + a * H, H)], start=(a == 0), stop=(a == 1))
                    ins.then_inc(m["d_done"], 1)

                def turn(base, group, first, last):
                    before = None if first else weights_of(base - 1)
                    off = weights_of(base)
                    for j in range(UNROLL):
                        s = base + j
                        early = first and j < 2
                        pe.wait_ge(m["xT_copied"], s + 1)
                        if not early:
                            pe.wait_ge(m["h_ready"], s - 1)
                        gate_up(j, 0, off)
                        if before is not None:
                            turn_h(s - 1, j - 1, first and j - 1 < 2)
                        if not (last and j == UNROLL - 1):
                            turn_in(s + 1, j + 1, group, first and j + 1 < 2)
                        gate_up(j, 1, off).then_inc(m["g_done"], 1)
                        after = weights_of(s + 1) if j + 1 < UNROLL else None
                        if before is not None:
                            down(s - 1, j - 1, before, first and j - 1 < 2)
                        before, off = off, after
                    if last:
                        turn_h(base + UNROLL - 1, UNROLL - 1, False)
                        down(base + UNROLL - 1, UNROLL - 1, before, False)

                turn_in(0, 0, 0, True)
                turns(pe, L, turn)

            pe.wait_ge(small_in, 64)
            routing(L0, rw0, (w_shared, 32))
            pe.wait_ge(w_early, 32 * -(-(L0.E - LATE) // EARLY))
            pe.wait_ge(w_late, 64)
            tiles(L0)


            KV = 16 * (1 + 2 * len(QK_PARTS) + 1)

            def scores(g):
                t = g // HPT
                pe.wait_ge(batch_in[t // 2], KV)
                pe.wait_ge(qs_in[t % 2], 128 * (t // 2 + 1))
                if g >= 4:
                    pe.wait_ge(p_raw, 2 * g - 6)
                for q in range(2):
                    for s_ in range(2):
                        ins = T.matmul(bank[g % 4][:, q * H:(q + 1) * H], qs[:, t % 2, s_, g % HPT, q * P:(q + 1) * P],
                                       ks[:, s_, g, :], start=(s_ == 0), stop=(s_ == 1))
                ins.then_inc(s_done, 1)

            def turn_p(g):
                pe.wait_ge(p_ready, g + 1)
                if g < ALONE:
                    pe.wait_ge(p2_ready, g + 1)
                if g >= ALONE:
                    pe.wait_ge(p1_ready, g + 1 - ALONE)
                if g >= 2:
                    pe.wait_ge(pT_ready, g - 1)
                for k in range(2):
                    for q in range(2):
                        ins = T.transpose(bank[4 + g % 2][:, (2 * k + q) * P:(2 * k + q + 1) * P],
                                          pr_sb[:, g % 4, q, k * P:(k + 1) * P], ident[:])
                ins.then_inc(tp_done, 1)

            def values(g):
                t, r0 = g // HPT, (g % HPT) * HEAD
                pe.wait_ge(batch_in[t // 2], KV)
                pe.wait_ge(pT_ready, g + 1)
                if t >= 2:
                    pe.wait_ge(x3_ready, t - 1)
                for k in range(2):
                    row = (t % 2) * P + r0
                    ins = T.matmul(bank[6 + t % 2][r0:r0 + HEAD, 0:H], vT[:, t // 2, k, row:row + HEAD],
                                   pT_sb[:, g % 2, k, :], start=(k == 0), stop=(k == 1), tile_position=(0, r0))
                ins.then_inc(av_done, 1)

            for g in range(3):
                scores(g)
            for g in range(nheads + 1):
                if g + 3 < nheads:
                    scores(g + 3)
                if g < nheads:
                    turn_p(g)
                if g >= 1:
                    values(g - 1)
            routing(L1, rw1, (w1_in, 96))
            tiles(L1)
            shared_steps(L1, "after", n_mid["m1"], len(after_work["m1"]), n_mid["m1"], len(after_work["m1"]) + 1)


def kernel(**inputs):
    import numpy as np
    import concourse.bacc as bacc
    from concourse.bass_utils import run_bass_kernel_spmd

    a = {k: np.asarray(v) for k, v in inputs.items()}

    def chunks(w):
        n, h = w.shape
        return np.ascontiguousarray(w.T.reshape(h // P, P, n).transpose(1, 0, 2))

    def experts(gate, up, down):
        e, i, h = gate.shape
        gu = np.concatenate([gate, up], axis=1).transpose(2, 0, 1).reshape(h // P, P, e, 2 * i).transpose(1, 2, 0, 3)
        dn = down.transpose(2, 0, 1).reshape(2, i // 2, e, h).transpose(1, 2, 0, 3)
        return np.ascontiguousarray(gu.reshape(P, e, -1)), np.ascontiguousarray(dn.reshape(i // 2, e, -1))

    def halves(w, i, axis):
        return np.stack(np.split(w, w.shape[axis] // i, axis=axis))

    i0 = a["L0_ffn_gate_w"].shape[1]
    gu0, dn0 = experts(*(np.concatenate([halves(a["L0_ffn_shared_" + n], i0, ax), a["L0_ffn_" + n]])
                         for n, ax in (("gate_w", 0), ("up_w", 0), ("down_w", 1))))
    i1 = a["L1_ffn_w1"].shape[1]
    gu1, dn1 = experts(*(np.concatenate([halves(a["L1_ffn_s" + n], i1, ax), a["L1_ffn_" + n]])
                         for n, ax in (("w1", 0), ("w2", 0), ("w3", 1))))
    x = a["x"]
    H = x.shape[2]
    arrays = {
        "x": x.reshape(-1, P, H), "ctx": a["ctx_2048"], "ctxT": np.ascontiguousarray(a["ctx_2048"].transpose(0, 2, 1)),
        "router_w0": chunks(a["L0_ffn_router_w"]), "router_b0": a["L0_ffn_router_b"].reshape(1, -1),
        "w_gu0": gu0, "w_dn0": dn0, "gamma": a["L1_xattn_gamma"].reshape(1, 1),
        "router_w1": chunks(a["L1_ffn_gate_w"]), "w_gu1": gu1, "w_dn1": dn1,
    }
    arrays = {k: np.ascontiguousarray(v) for k, v in arrays.items()}
    nc = bacc.Bacc("TRN2", target_bir_lowering=False, num_devices=1)
    args = [nc.dram_tensor(n, v.shape, mybir.dt.from_np(v.dtype), kind="ExternalInput").ap() for n, v in arrays.items()]
    out = nc.dram_tensor("out", arrays["x"].shape, F32, kind="ExternalOutput").ap()
    mk_xattn_ffn(nc, *args, out)
    r = run_bass_kernel_spmd(nc, [arrays], core_ids=[0])
    return r.results[0]["out"].reshape(x.shape)
```

```python
from contextlib import ExitStack

import numpy as np
import concourse.bass as bass
from concourse import mybir

ALU = mybir.AluOpType
ACT = mybir.ActivationFunctionType
AX = mybir.AxisListType
F32 = mybir.dt.float32
F16 = mybir.dt.float16
BF16 = mybir.dt.bfloat16
I32 = mybir.dt.int32
U32 = mybir.dt.uint32

P = 128
LN_EPS = 1e-5
FP8_MAX = 448.0
ACT_EPS = 1e-4
W_EPS = 1e-6
ROUTED_SCALE = 1.8
BUFS = 4
EARLY = 9
HEAD = 32


class Moe:

    def __init__(self, name, E, K, half, shared, n_tok, unroll):
        self.name, self.E, self.K, self.J, self.S = name, E, K, half, shared
        most = (n_tok * K + (P - 1) * E) // P
        self.unroll = unroll
        self.tiles = -(-most // unroll) * unroll
        self.gu = 2 * 2 * 2 * half


def mk_xattn_ffn(nc, x, ctx, ctxT, router_w0, router_b0, w_gu0, w_dn0, gamma, router_w1, w_gu1, w_dn1, out):
    NT, _, H = x.shape
    C = H // P
    n_tok = NT * P
    NB = ctx.shape[0]
    HPT = P // HEAD
    nheads = NT * HPT
    SCALE = float(HEAD) ** -0.5
    L0 = Moe("m0", router_w0.shape[2], 4, w_dn0.shape[0], 1, n_tok, 16)
    L1 = Moe("m1", router_w1.shape[2], 2, w_dn1.shape[0], 2, n_tok, 8)
    for L in (L0, L1):
        L.stride = L.gu + 2 * H

    with ExitStack() as es:
        def sb(name, shape, dt=F32):
            return es.enter_context(nc.sbuf_tensor(name, shape, dt))

        def sem(name):
            return es.enter_context(nc.semaphore(name))

        bank = [es.enter_context(nc.psum_tensor(f"bank{i}", [P, 512], F32)) for i in range(8)]

        W_COLS = (L0.S + L0.E) * L0.stride
        arena = sb("arena", [P, W_COLS])
        x_sb = sb("x_sb", [P, NT, H])
        xn = sb("xn", [P, NT, H])
        ident = sb("ident", [P, P])
        ident16 = sb("ident16", [P, P], BF16)
        tri16 = sb("tri16", [P, P], BF16)
        tri_in16 = sb("tri_in16", [P, P], BF16)
        ones16 = sb("ones16", [P, P], BF16)
        ones32 = sb("ones32", [P, P])
        iota16 = sb("iota16", [P, P], F16)
        iota_e = sb("iota_e", [P, L0.E])
        thr = sb("thr", [P, NT])
        tokid = sb("tokid", [P, NT])
        gamma_sb = sb("gamma_sb", [P, 1])
        rw0 = sb("rw0", [P, C, L0.E])
        rb0 = sb("rb0", [P, L0.E])
        rw1 = sb("rw1", [P, C, L1.E])
        xg = sb("xg", [P, BUFS, H])
        xT = sb("xT", [P, 2, C, P])
        sg = sb("sg", [P, 2, 2 * L0.J])
        up = sb("up", [P, 2, 2 * L0.J])
        hh = sb("hh", [P, 2, 2 * L0.J])
        hT = sb("hT", [P, 2, 2, P])
        ysb = sb("ysb", [P, BUFS, H])
        gidx = sb("gidx", [P, BUFS], U32)
        st = sb("st", [P, NT, 6])
        mv = sb("mv", [P, NT, 2])
        ve = sb("ve", [P, NT])
        nt = sb("nt", [P, NT])
        rstd = sb("rstd", [P, NT])
        amc = sb("amc", [P, 16])
        amx = sb("amx", [P, 16])
        col16 = sb("col16", [P, 1])
        diag = sb("diag", [P, 16])
        safe_c = sb("safe_c", [P, 16])
        rin_c = sb("rin_c", [P, 16])
        rin_x = sb("rin_x", [P, 16])
        dq = sb("dq", [P, NT, C, C])
        small = {L0.name: {}, L1.name: {}}

        def routed(name, shape_of, dt=F32, rows=P):
            flat = sb(name, [rows, max(int(np.prod(shape_of(L))) for L in (L0, L1))], dt)
            for L in (L0, L1):
                shape = shape_of(L)
                v = flat[:, 0:int(np.prod(shape))]
                small[L.name][name] = v.rearrange("p (t k) -> p t k", t=shape[0]) if len(shape) == 2 else v

        routed("lg", lambda L: (NT, L.E))
        routed("m16", lambda L: (NT, L.E), BF16)
        for n in ("top", "idxf"):
            routed(n, lambda L: (NT, 8))
        routed("idx", lambda L: (NT, 8), U32)
        for n, dt in (("rw", F32), ("slotf", F32), ("tf", F32), ("pf", F32), ("sloti", I32), ("ti", I32), ("pi", I32),
                      ("back", U32)):
            routed(n, lambda L: (NT, L.K), dt)
        for n in ("s1", "s2", "junk"):
            routed(n, lambda L: (NT,))
        for n in ("cnt", "ntc", "endc"):
            routed(n, lambda L: (1,))
        routed("ntr", lambda L: (P,), BF16)
        routed("cmp", lambda L: (L.tiles,), BF16)
        routed("startb", lambda L: (L.E,))
        routed("tab", lambda L: (L.tiles,), U32)
        routed("te", lambda L: (L.tiles,), rows=1)
        routed("etab", lambda L: (L.tiles,), I32, rows=1)
        for n in ("nm", "rsum", "rinv"):
            small[n] = sb("att_" + n, [P, 4, 2])

        def part(at, cols):
            return arena[:, at:at + cols], at + cols

        LATE = 4
        late0 = (W_COLS // L0.stride - LATE) * L0.stride
        at = late0
        v_c, at = part(at, NB * C * H)
        c_c, at = part(at, NB * C * H)
        wq, at = part(at, NB * C * H // 2)
        assert at <= W_COLS
        wq = wq.bitcast(BF16).rearrange("p (b k n) -> p b k n", b=NB, k=C)
        v_x = xn[:].rearrange("p t h -> p (t h)")
        qx = ysb[:].rearrange("p s h -> p (s h)").bitcast(BF16)
        xqT = xg[:].rearrange("p s h -> p (s h)").bitcast(BF16).rearrange("p (t k m) -> p t k m", t=NT, k=C)
        L1_SCRATCH_AT, BACK_AT = 20000, 30000
        RS = {}
        for L, at in ((L0, late0), (L1, L1_SCRATCH_AT)):
            d = {}
            n = NT * L.K * L.E
            d["oh"], at0 = part(at, n)
            d["pr"], at0 = part(at0, n)
            d["base"], at0 = part(at0, NT * L.E)
            d["pos1"], at = part(at, NT * L.K * P // 2)
            d["til1"], at = part(at, NT * L.K * L.tiles // 2)
            at = max(at, at0)
            last = -(-(W_COLS - at) // L0.stride)
            d["xT"], at = part(at, NT * H)
            d["last"] = last
            d["xT"] = d["xT"].rearrange("p (t c m) -> p t c m", t=NT, c=C)
            d["oh"] = d["oh"].rearrange("p (t k e) -> p t k e", t=NT, k=L.K)
            d["pr"] = d["pr"].rearrange("p (t k e) -> p t k e", t=NT, k=L.K)
            d["base"] = d["base"].rearrange("p (t e) -> p t e", t=NT)
            d["pos1"] = d["pos1"].bitcast(F16).rearrange("p (a m) -> p a m", m=P)
            d["til1"] = d["til1"].bitcast(F16).rearrange("p (a m) -> p a m", m=L.tiles)
            assert at <= W_COLS
            RS[L.name] = d
        at = 0
        _, at = part(at, (L1.S + L1.E) * L1.stride)
        vT, at = part(at, NB * C * H)
        vT = vT.rearrange("p (b k n) -> p b k n", b=NB, k=C)
        pr_sb, at = part(at, 4 * 2 * H)
        pT_sb, at = part(at, 2 * 2 * H)
        pr_sb = pr_sb.rearrange("p (b q k) -> p b q k", b=4, q=2)
        pT_sb = pT_sb.rearrange("p (b k q) -> p b k q", b=2, k=2)
        QK_PARTS = (((0, 0), (0, 2)), ((0, 2), (1, 0)), ((1, 1), (0, 2)), ((1, 2), (1, 1)))
        ks, at = part(at, 2 * nheads * H // 2)
        ks = ks.bitcast(BF16).rearrange("p (s g n) -> p s g n", s=2, g=nheads)
        qs, at = part(at, 2 * 2 * HPT * H // 2)
        qs = qs.bitcast(BF16).rearrange("p (b s g n) -> p b s g n", b=2, s=2, g=HPT)
        q3, at = part(at, 2 * 3 * H // 2)
        q3 = q3.bitcast(BF16).rearrange("p (b a n) -> p b a n", b=2, a=3)
        k_raw, at1 = part((L0.S + 2 * EARLY) * L0.stride, NT * H)
        k3, at1 = part(at1, 3 * NT * H // 2)
        k3 = k3.bitcast(BF16).rearrange("p (a m) -> p a m", a=3)
        c_x, at1 = part(at1, NT * H)
        assert at1 <= (L0.S + 3 * EARLY) * L0.stride
        assert at <= BACK_AT
        back_rows = {}
        at = BACK_AT
        for L in (L0, L1):
            r, _ = part(at, NT * L.K * H)
            back_rows[L.name] = r.rearrange("p (t k h) -> p t k h", t=NT, k=L.K)
            assert at + NT * L.K * H <= W_COLS

        xn_d = {L.name: nc.dram_tensor(L.name + "_xn", (n_tok, H), F32, kind="Internal").ap() for L in (L0, L1)}
        ys_d = {L.name: nc.dram_tensor(L.name + "_ys", (L.tiles * P, H), F32, kind="Internal").ap() for L in (L0, L1)}

        k3_d = nc.dram_tensor("k3_d", (HEAD, 3, nheads, H), BF16, kind="Internal").ap()
        q3_d = nc.dram_tensor("q3_d", (NT, HEAD, 3, HPT, H), BF16, kind="Internal").ap()

        batch_in = [sem(f"batch_in{b}") for b in range(NB)]
        ctxT_in = sem("ctxT_in")
        k_raw_in, k3_ready, k3_stored = sem("k_raw_in"), sem("k3_ready"), sem("k3_stored")
        q3_ready, q3_stored, qs_in = sem("q3_ready"), sem("q3_stored"), [sem(f"qs_in{i}") for i in range(2)]
        small_in = sem("small_in")
        w_shared, w_early, w_late, w1_in = sem("w_shared"), sem("w_early"), sem("w_late"), sem("w1_in")
        consts = sem("consts")
        dve_step = sem("dve_step")
        pool_step = sem("pool_step")
        amc_ready, amcT_done, diag_ready, amb_done = (sem(n) for n in ("amc_ready", "amcT_done", "diag_ready", "amb_done"))
        c_mag, wq_ready, xq_ready, xqT_done, xqT_sb, xp_done, x1_ready = (
            sem(n) for n in ("c_mag", "wq_ready", "xq_ready", "xqT_done", "xqT_sb", "xp_done", "x1_ready"))

        rows_back = [sem(f"rows_back{t}") for t in range(NT)]
        rows_in = {L0.name: 16 * L0.K, L1.name: 16 * (L0.K + L1.K)}
        M = {}
        for L in (L0, L1):
            m = {n: sem(f"{L.name}_{n}") for n in (
                "xn_ready xn_stored rt_T rt_Tsb logits exp_in exp_out mask counts ntiles starts "
                "cmp owner table_e onehots tokens table idx_col idx_seen t_done xT_copied g_done "
                "sg_ready h_ready ht_done hT_copied d_done y_copied ").split()}
            m["xg_in"] = [sem(f"{L.name}_xg_in{i}") for i in range(BUFS)]
            m["y_stored"] = [sem(f"{L.name}_y_stored{i}") for i in range(BUFS)]
            m["early"] = {n: sem(f"{L.name}_early_{n}") for n in
                          "g_done evacuated h_ready ht_done hT_copied d_done y_copied added".split()}
            m["after"] = {n: sem(f"{L.name}_after_{n}") for n in
                          "g_done evacuated h_ready ht_done hT_copied d_done added".split()}
            M[L.name] = m
        x2_ready, s_done, nm_ready, p_raw, p_ready, tp_done, pT_ready, av_done, x3_ready = (
            sem(n) for n in ("x2_ready", "s_done", "nm_ready", "p_raw", "p_ready", "tp_done", "pT_ready", "av_done", "x3_ready"))
        rinv_ready, p1_ready, p2_ready = sem("rinv_ready"), sem("p1_ready"), sem("p2_ready")
        stats_ready, rstd_ready = sem("stats_ready"), sem("rstd_ready")
        out_ready, stored = sem("out_ready"), sem("stored")

        block = es.enter_context(nc.Block())
        ALONE = 8

        def turns(eng, L, turn):
            n = L.tiles // L.unroll
            turn(0, 0, True, False)
            with eng.Fori(1, n - 1) as g:
                turn(g * L.unroll, g, False, False)
            turn((n - 1) * L.unroll, n - 1, False, True)

        every = {L.name: [(i, t) for i in range(L.S) for t in range(NT)] for L in (L0, L1)}
        n_early = {"m0": 5, "m1": 2}
        n_mid = {"m0": 3, "m1": 3}
        early_work = {n: every[n][:n_early[n]] for n in every}
        after_work = {n: every[n][n_early[n]:] for n in every}

        def inverse_deviation(engine, link, tiles, scale):
            a, b = tiles[0], tiles[-1] + 1
            h, r, w = ve[:, a:b], rstd[:, a:b], nt[:, a:b]
            link(engine.tensor_scalar(h, mv[:, a:b, 1], LN_EPS, -0.5 / scale ** 2, ALU.add, ALU.mult))
            link(engine.tensor_scalar(r.bitcast(I32), h.bitcast(I32), -0.5, float(0x5F3759DF - 2 ** 30 - 2 ** 22),
                                      ALU.mult, ALU.add))
            for _ in range(3):
                link(engine.tensor_tensor(w, h, r, ALU.mult))
                link(engine.tensor_tensor(w, w, r, ALU.mult))
                if engine is nc.vector:
                    link(engine.scalar_tensor_tensor(out=r, in0=w, scalar=1.5, in1=r, op0=ALU.add, op1=ALU.mult))
                else:
                    link(engine.tensor_scalar(w, w, 1.5, None, ALU.add))
                    link(engine.tensor_tensor(r, w, r, ALU.mult))

        by_pool = {5: ((4, 5), SCALE), 10: ((0, 1), 1.0), 13: ((6, 7), SCALE), 18: ((2, 3), 1.0), 26: ((4, 5), 1.0)}

        @block.sync
        def _(sp):
            for t in range(0, NT, 2):
                sp.dma_start(x_sb[:, t:t + 2, :], x[t:t + 2].rearrange("t p h -> p t h")).then_inc(batch_in[t // 2], 16)
            n0 = L0.S + L0.E

            def experts(L, a, b, w_gu, w_dn, done):
                w = arena[:, a * L.stride:b * L.stride].rearrange("p (e c) -> p e c", c=L.stride)
                sp.dma_start(w[:, :, 0:L.gu], w_gu[:, a:b, :]).then_inc(done, 16)
                sp.dma_start(w[0:L.J, :, L.gu:L.stride], w_dn[:, a:b, :]).then_inc(done, 16)

            def store_xn(L):
                m = M[L.name]
                sp.wait_ge(m["xn_ready"], NT)
                sp.dma_start(xn_d[L.name].rearrange("(t p) h -> p t h", p=P), xn[:]).then_inc(m["xn_stored"], 16)

            def store_tiles(L):
                m = M[L.name]

                def turn(base, group, first, last):
                    for j in range(L.unroll):
                        sp.wait_ge(m["y_copied"], base + j + 1)
                        b = j % BUFS
                        sp.dma_start(ys_d[L.name][bass.ds((base + j) * P, P), :], ysb[:, b, :]).then_inc(m["y_stored"][b], 16)

                turns(sp, L, turn)
                for b in range(BUFS):
                    sp.wait_ge(m["y_stored"][b], 16 * (L.tiles // BUFS))

            sp.wait_ge(ctxT_in, 16)
            experts(L0, 0, L0.S, w_gu0, w_dn0, w_shared)
            sp.dma_start(k_raw.rearrange("p (t n) -> p t n", t=NT), ctx.rearrange("b (k p) n -> p (b k) n", p=P)).then_inc(k_raw_in, 16)
            for i, a in enumerate(range(L0.S, n0 - LATE, EARLY)):
                if i == 2:
                    sp.wait_ge(k3_ready, 1)
                    sp.wait_ge(xq_ready, 2)
                    for h in range(HPT):
                        for a_ in range(3):
                            sp.dma_start(k3_d[:, a_, h:nheads:HPT, :], k3[h * HEAD:(h + 1) * HEAD, a_].rearrange(
                                "p (t n) -> p t n", t=NT)).then_inc(k3_stored, 16)
                    sp.wait_ge(k3_stored, 16 * 3 * HPT)
                experts(L0, a, min(a + EARLY, n0 - LATE), w_gu0, w_dn0, w_early)
            store_xn(L0)
            last = RS["m0"]["last"]
            sp.wait_ge(M["m0"]["table"], 1)
            experts(L0, n0 - LATE, n0 - last, w_gu0, w_dn0, w_late)
            sp.wait_ge(M["m0"]["early"]["g_done"], n_early["m0"])
            sp.wait_ge(M["m0"]["after"]["g_done"], n_mid["m0"])
            experts(L0, n0 - last, n0, w_gu0, w_dn0, w_late)
            store_tiles(L0)
            sp.wait_ge(M["m0"]["d_done"], L0.tiles)
            def places(dst, src, which, done):
                for i, parts in enumerate(QK_PARTS):
                    a, b = parts[which]
                    place = dst[i * HEAD:(i + 1) * HEAD].rearrange("p s g n -> p s (g n)")
                    if a < b:
                        sp.dma_start(place, src[:, a:b + 1:b - a, :]).then_inc(done, 16)
                    elif a == b:
                        sp.dma_start(place, src[:, a:a + 1, :].broadcast_to([HEAD, 2, src.shape[2]])).then_inc(done, 16)
                    else:
                        sp.dma_start(place[:, 0], src[:, a, :]).then_inc(done, 16)
                        sp.dma_start(place[:, 1], src[:, b, :]).then_inc(done, 16)

            def q_places(t):
                sp.wait_ge(q3_ready, t + 1)
                for h in range(HPT):
                    sp.dma_start(q3_d[t, :, :, h, :], q3[h * HEAD:(h + 1) * HEAD, t % 2]).then_inc(q3_stored, 16)
                sp.wait_ge(q3_stored, 16 * HPT * (t + 1))
                if t >= 2:
                    sp.wait_ge(s_done, HPT * (t - 1))
                places(qs[:, t % 2], q3_d[t].rearrange("r a g n -> r a (g n)"), 0, qs_in[t % 2])

            def kv(b):
                heads = slice(2 * b * HPT, 2 * (b + 1) * HPT)
                places(ks[:, :, heads], k3_d[:, :, heads, :].rearrange("r a g n -> r a (g n)"), 1, batch_in[b])
                sp.dma_start(vT[:, b], ctxT[b].rearrange("(k p) n -> p k n", p=P)).then_inc(batch_in[b], 16)

            sp.wait_ge(rows_back[0], rows_in["m0"])
            kv(0)
            q_places(0)
            q_places(1)
            kv(1)
            q_places(2)
            q_places(3)
            kv(2)
            kv(3)
            q_places(4)
            for t in range(NT):
                sp.wait_ge(rows_back[t], rows_in["m0"])
            cuts = [(L1.S + L1.E) * i // 3 for i in range(4)]
            for i in range(3):
                q_places(5 + i)
                experts(L1, cuts[i], cuts[i + 1], w_gu1, w_dn1, w1_in)
            store_xn(L1)
            store_tiles(L1)
            for t in range(NT):
                sp.wait_ge(out_ready, t + 1)
                sp.dma_start(out[t], x_sb[:, t, :]).then_inc(stored, 16)
            sp.wait_ge(stored, 16 * NT)

        @block.gpsimd
        def _(pool):
            step = [0]

            def link(ins):
                step[0] += 1
                ins.then_inc(pool_step, 1)
                pool.wait_ge(pool_step, step[0])

            link(nc.gpsimd.memset(ident[:], 0.0))
            link(nc.gpsimd.memset(ident16[:], 0.0))
            link(nc.gpsimd.memset(ones16[:], 1.0))
            link(nc.gpsimd.memset(ones32[:], 1.0))
            for i in (ident, ident16):
                nc.gpsimd.affine_select(out=i[:], in_=i[:], compare_op=ALU.not_equal, fill=1.0, base=0,
                                        pattern=[[-1, P]], channel_multiplier=1).then_inc(consts, 1)
            nc.gpsimd.affine_select(out=tri16[:], in_=ones16[:], compare_op=ALU.is_gt, fill=0.0, base=0,
                                    pattern=[[1, P]], channel_multiplier=-1).then_inc(consts, 1)
            nc.gpsimd.affine_select(out=tri_in16[:], in_=ones16[:], compare_op=ALU.is_ge, fill=0.0, base=0,
                                    pattern=[[1, P]], channel_multiplier=-1).then_inc(consts, 1)
            for buf, pattern, rows in ((iota16, [[1, P]], 0), (iota_e, [[1, L0.E]], 0), (thr, [[P, NT]], 0),
                                       (tokid, [[P, NT]], 1)):
                nc.gpsimd.iota(buf[:], pattern, base=0, channel_multiplier=rows,
                               allow_small_or_imprecise_dtypes=True).then_inc(consts, 1)

            pool.wait_ge(c_mag, 1)
            link(nc.gpsimd.tensor_tensor(v_c, v_c, c_c, ALU.add))
            nc.gpsimd.tensor_tensor(wq.rearrange("p b k n -> p (b k n)"), v_c, c_c, ALU.subtract).then_inc(wq_ready, 1)

            pool.wait_ge(k_raw_in, 16)
            link(nc.gpsimd.tensor_copy(k3[:, 0], k_raw))
            link(nc.gpsimd.tensor_tensor(k_raw, k_raw, k3[:, 0], ALU.subtract))
            link(nc.gpsimd.tensor_copy(k3[:, 1], k_raw))
            nc.gpsimd.tensor_tensor(k3[:, 2], k_raw, k3[:, 1], ALU.subtract).then_inc(k3_ready, 1)

            def early_shared(L):
                q, work = M[L.name]["early"], early_work[L.name]
                for n in range(len(work) + 1):
                    if n < len(work):
                        pool.wait_ge(q["evacuated"], n + 1)
                        if n >= 2:
                            pool.wait_ge(q["ht_done"], n - 1)
                        nc.gpsimd.tensor_tensor(hh[:, n % 2, 0:2 * L.J], sg[:, n % 2, 0:2 * L.J], up[:, n % 2, 0:2 * L.J],
                                                ALU.mult).then_inc(q["h_ready"], 1)
                    if n >= 1:
                        t = work[n - 1][1]
                        pool.wait_ge(q["y_copied"], n)
                        nc.gpsimd.tensor_tensor(x_sb[:, t, :], x_sb[:, t, :], ysb[:, (n - 1) % 2, :],
                                                ALU.add).then_inc(q["added"], 1)

            def gathers(L):
                m, d = M[L.name], small[L.name]
                pool.wait_ge(m["xn_stored"], 16)
                pool.wait_ge(m["table"], 1)

                def turn(base, group, first, last):
                    for j in range(L.unroll):
                        s, b = base + j, j % BUFS
                        if not first or j >= BUFS:
                            pool.wait_ge(m["t_done"], s - BUFS + 1)
                        nc.gpsimd.tensor_copy(gidx[:, b:b + 1], d["tab"][:, bass.ds(s, 1)]).then_inc(m["idx_col"], 1)
                        pool.wait_ge(m["idx_col"], s + 1)
                        pool.sem_inc(m["idx_seen"], 1)
                        nc.gpsimd.indirect_dma_start(
                            out=xg[:, b, :], out_offset=None, in_=xn_d[L.name],
                            in_offset=bass.IndirectOffsetOnAxis(ap=gidx[:, b:b + 1], axis=0)).then_inc(m["xg_in"][b], 16)

                turns(pool, L, turn)

            def gather_back(L):
                m, d = M[L.name], small[L.name]
                for b in range(BUFS):
                    pool.wait_ge(m["y_stored"][b], 16 * (L.tiles // BUFS))
                for t in range(NT):
                    for k in range(L.K):
                        nc.gpsimd.indirect_dma_start(
                            out=back_rows[L.name][:, t, k, :], out_offset=None, in_=ys_d[L.name],
                            in_offset=bass.IndirectOffsetOnAxis(ap=d["back"][:, t, k:k + 1], axis=0)
                        ).then_inc(rows_back[t], 16)

            def head_norm(g):
                pool.wait_ge(rinv_ready, g + 1)
                nc.gpsimd.tensor_scalar(pr_sb[:, g % 4, 1, :], pr_sb[:, g % 4, 1, :], small["rinv"][:, g % 4, 1:2],
                                        None, ALU.mult).then_inc(p1_ready, 1)

            early_shared(L0)
            gathers(L0)
            gather_back(L0)
            for g in range(nheads):
                if g - 2 in by_pool:
                    pool.wait_ge(stats_ready, sum(k <= g - 2 for k in by_pool))
                    inverse_deviation(nc.gpsimd, link, *by_pool[g - 2])
                    pool.sem_inc(rstd_ready, 1)
                if g >= ALONE:
                    head_norm(g)
            early_shared(L1)
            gathers(L1)
            gather_back(L1)

        @block.scalar
        def _(act):
            act.dma_start(v_c.rearrange("p (b k n) -> p b k n", b=NB, k=C),
                          ctxT.rearrange("b (k p) n -> p b k n", p=P)).then_inc(ctxT_in, 16)
            act.dma_start(rw0[:], router_w0).then_inc(small_in, 16)
            act.dma_start(rb0[:], router_b0.to_broadcast([P, L0.E])).then_inc(small_in, 16)
            act.dma_start(rw1[:], router_w1).then_inc(small_in, 16)
            act.dma_start(gamma_sb[:], gamma.to_broadcast([P, 1])).then_inc(small_in, 16)

            for i in range(2):
                act.wait_ge(xqT_done, i + 1)
                nc.scalar.activation(xqT[:, 4 * i:4 * i + 4].rearrange("p t k m -> p (t k m)"),
                                     bank[i][:].bitcast(BF16), ACT.Copy).then_inc(xqT_sb, 1)

            def router_copies(L, pairs):
                m = M[L.name]
                for i in pairs:
                    act.wait_ge(m["rt_T"], i + 1)
                    nc.scalar.activation(RS[L.name]["xT"][:, 2 * i:2 * i + 2].rearrange("p t c m -> p (t c m)"),
                                         bank[i % 2][:], ACT.Copy).then_inc(m["rt_Tsb"], 1)

            def hT_out(L, q, n):
                act.wait_ge(q["ht_done"], n + 1)
                if n >= 2:
                    act.wait_ge(q["d_done"], n - 1)
                nc.scalar.activation(hT[0:L.J, n % 2].rearrange("p a m -> p (a m)"), bank[6][0:L.J, 0:2 * P],
                                     ACT.Copy).then_inc(q["hT_copied"], 1)

            def early_shared(L):
                q, J2, N = M[L.name]["early"], 2 * L.J, len(early_work[L.name])
                for n in range(N + 1):
                    if n >= 1:
                        hT_out(L, q, n - 1)
                    if n < N:
                        act.wait_ge(q["g_done"], n + 1)
                        if n >= 2:
                            act.wait_ge(q["h_ready"], n - 1)
                        nc.scalar.activation(sg[:, n % 2, 0:J2], bank[4 + n % 2][:, 0:J2], ACT.Silu)
                        nc.scalar.activation(up[:, n % 2, 0:J2], bank[4 + n % 2][:, J2:2 * J2],
                                             ACT.Copy).then_inc(q["evacuated"], 1)
                    if n >= 1:
                        act.wait_ge(q["d_done"], n)
                        if n >= 3:
                            act.wait_ge(q["added"], n - 2)
                        nc.scalar.activation(ysb[:, (n - 1) % 2, :], bank[7][:, 0:H], ACT.Copy).then_inc(q["y_copied"], 1)

            def after_shared(L, a, b):
                q, J2 = M[L.name]["after"], 2 * L.J
                for n in range(a, b + 1):
                    if n > a:
                        hT_out(L, q, n - 1)
                    if n < b:
                        act.wait_ge(q["g_done"], n + 1)
                        if n >= 2:
                            act.wait_ge(q["h_ready"], n - 1)
                        nc.scalar.activation(sg[:, n % 2, 0:J2], bank[4 + n % 2][:, 0:J2],
                                             ACT.Silu).then_inc(q["evacuated"], 1)

            def tiles(L):
                m = M[L.name]

                def xT_copy(s, j, early):
                    act.wait_ge(m["t_done"], s + 1)
                    if not early:
                        act.wait_ge(m["g_done"], s - 1)
                    nc.scalar.activation(xT[:, j % 2].rearrange("p c m -> p (c m)"), bank[j % 2][:, 0:H],
                                         ACT.Copy).then_inc(m["xT_copied"], 1)

                def turn(base, group, first, last):
                    if first:
                        xT_copy(0, 0, True)
                    for j in range(L.unroll):
                        s = base + j
                        if not (last and j == L.unroll - 1):
                            xT_copy(s + 1, j + 1, first and j + 1 < 2)
                        act.wait_ge(m["g_done"], s + 1)
                        if not first or j >= 2:
                            act.wait_ge(m["h_ready"], s - 1)
                        nc.scalar.activation(sg[:, j % 2, 0:2 * L.J], bank[2 + j % 2][:, 0:2 * L.J],
                                             ACT.Silu).then_inc(m["sg_ready"], 1)

                turns(act, L, turn)

            router_copies(L0, range(NT // 2))
            early_shared(L0)
            after_shared(L0, 0, n_mid["m0"])
            tiles(L0)

            act.wait_ge(M["m0"]["exp_in"], 1)
            nc.scalar.activation(small["m0"]["rw"][:], small["m0"]["rw"][:], ACT.Exp).then_inc(M["m0"]["exp_out"], 1)

            def softmax_exp(g):
                act.wait_ge(nm_ready, g + 1)
                if g >= 4:
                    act.wait_ge(tp_done, g - 3)
                for q in range(2):
                    nc.scalar.activation(pr_sb[:, g % 4, q, :], bank[g % 4][:, q * H:(q + 1) * H], ACT.Exp,
                                         bias=small["nm"][:, g % 4, q:q + 1],
                                         accum_out=small["rsum"][:, g % 4, q:q + 1]).then_inc(p_raw, 1)

            def pT_copy(g):
                act.wait_ge(tp_done, g + 1)
                if g >= 2:
                    act.wait_ge(av_done, g - 1)
                nc.scalar.activation(pT_sb[:, g % 2].rearrange("p k q -> p (k q)"), bank[4 + g % 2][:],
                                     ACT.Copy).then_inc(pT_ready, 1)

            def divide(g):
                act.wait_ge(rinv_ready, g + 1)
                nc.scalar.activation(pr_sb[:, g % 4, 0, :], pr_sb[:, g % 4, 0, :], ACT.Copy,
                                     scale=small["rinv"][:, g % 4, 0:1]).then_inc(p_ready, 1)

            for g in range(3):
                softmax_exp(g)
            divide(0)
            divide(1)
            for g in range(nheads):
                pT_copy(g)
                if g == nheads - 1:
                    router_copies(L1, [0])
                if g + 2 < nheads:
                    divide(g + 2)
                if g + 3 < nheads:
                    softmax_exp(g + 3)
            router_copies(L1, range(1, NT // 2))
            act.wait_ge(M["m1"]["exp_in"], 1)
            nc.scalar.activation(small["m1"]["lg"][:], small["m1"]["lg"][:], ACT.Exp).then_inc(M["m1"]["exp_out"], 1)
            early_shared(L1)
            after_shared(L1, 0, n_mid["m1"])
            tiles(L1)
            after_shared(L1, n_mid["m1"], len(after_work["m1"]))

        @block.vector
        def _(dve):
            step = [0]

            def link(ins):
                step[0] += 1
                ins.then_inc(dve_step, 1)
                dve.wait_ge(dve_step, step[0])

            V = nc.vector

            def statistics(tiles, arrived=None):
                for t in tiles:
                    if arrived is not None and t % 2 == 0:
                        dve.wait_ge(arrived[t // 2], 16)
                    ins = V.bn_stats(st[:, t, :], x_sb[:, t, :])
                link(ins)
                for t in tiles:
                    ins = V.bn_aggr(mv[:, t, :], st[:, t, :])
                return ins

            def normalise(tiles, done=None):
                for t in tiles:
                    ins = V.tensor_scalar(xn[:, t, :], x_sb[:, t, :], mv[:, t, 0:1], rstd[:, t:t + 1],
                                          ALU.subtract, ALU.mult)
                    if done is not None:
                        ins.then_inc(done, 1)
                return ins

            def layernorm(tiles, done=None):
                link(statistics(tiles))
                inverse_deviation(V, link, tiles, 1.0)
                return normalise(tiles, done)

            def power_of_two(c, v):
                link(V.tensor_scalar(c.bitcast(I32), v.bitcast(I32), 0x7F800000, None, ALU.bitwise_and))
                return V.tensor_scalar(c, c, 2.0 ** -6, 1.5 * 2.0 ** 20, ALU.max, ALU.mult)

            link(statistics(range(NT // 2), batch_in))
            dve.wait_ge(ctxT_in, 16)
            ctx16 = v_c.rearrange("p (a n) -> p a n", n=P)
            V.tensor_reduce(amc[:], ctx16, AX.X, ALU.max, apply_absolute_value=True).then_inc(amc_ready, 1)
            link(statistics(range(NT // 2, NT), batch_in))
            dve.wait_ge(consts, 8)
            dve.wait_ge(amcT_done, 1)
            link(V.tensor_reduce(col16[0:16, :], bank[2][0:16, 0:P], AX.X, ALU.max))
            V.tensor_scalar(diag[0:16, :], ident[0:16, 0:16], col16[0:16, :], None, ALU.mult).then_inc(diag_ready, 1)
            inverse_deviation(V, link, range(NT), 1.0)
            dve.wait_ge(amb_done, 1)
            link(V.tensor_scalar(safe_c[:], bank[3][:, 0:16], W_EPS, None, ALU.max))
            link(V.reciprocal(rin_c[:], safe_c[:]))
            link(V.tensor_scalar(rin_c[:], rin_c[:], FP8_MAX, None, ALU.mult))
            link(V.tensor_tensor(ctx16, ctx16, rin_c[:].unsqueeze(2).broadcast_to([P, 16, P]), ALU.mult))
            power_of_two(c_c, v_c).then_inc(c_mag, 1)
            link(normalise(range(NT)))
            xn16 = v_x.rearrange("p (a n) -> p a n", n=P)
            link(V.tensor_reduce(amx[:], xn16, AX.X, ALU.max, apply_absolute_value=True))
            link(V.tensor_scalar(amx[:], amx[:], ACT_EPS, None, ALU.max))
            link(V.reciprocal(rin_x[:], amx[:]))
            link(V.tensor_scalar(rin_x[:], rin_x[:], FP8_MAX, None, ALU.mult))
            link(V.tensor_scalar(safe_c[:], safe_c[:], 1.0 / FP8_MAX, 1.0 / FP8_MAX, ALU.mult, ALU.mult))
            for t in range(NT):
                b = t // 2
                V.tensor_tensor(dq[:, t], amx[:, C * t:C * t + C].unsqueeze(2).broadcast_to([P, C, C]),
                                safe_c[:, 4 * b:4 * b + 4].rearrange("p (k n) -> p k n", k=C), ALU.mult)
            n = NT * H // 2
            for i in range(2):
                v, c = v_x[:, i * n:(i + 1) * n], c_x[:, i * n:(i + 1) * n]
                v16 = v.rearrange("p (a n) -> p a n", n=P)
                link(V.tensor_tensor(v16, v16, rin_x[:, 8 * i:8 * i + 8].unsqueeze(2).broadcast_to([P, 8, P]), ALU.mult))
                link(power_of_two(c, v))
                link(V.tensor_tensor(v, v, c, ALU.add))
                V.tensor_tensor(qx[:, i * n:(i + 1) * n], v, c, ALU.subtract).then_inc(xq_ready, 1)
            for t in range(NT):
                dve.wait_ge(xp_done, t + 1)
                for k in range(C):
                    for n in range(C):
                        ins = V.scalar_tensor_tensor(
                            out=x_sb[:, t, n * P:(n + 1) * P], in0=bank[4 + t % 2][:, k * H + n * P:k * H + (n + 1) * P],
                            scalar=dq[:, t, k, n:n + 1], in1=x_sb[:, t, n * P:(n + 1) * P], op0=ALU.mult, op1=ALU.add)
                        if n == C - 1 and k < C - 1:
                            link(ins)
                ins.then_inc(x1_ready, 1)
            dve.wait_ge(x1_ready, NT)

            def routing(L):
                m, d, r = M[L.name], small[L.name], RS[L.name]
                E, K = L.E, L.K
                dve.wait_ge(m["logits"], NT)
                lg = bank[2][:, 0:NT * E].rearrange("p (t e) -> p t e", t=NT)
                if L is L0:
                    dve.wait_ge(small_in, 64)
                    link(V.tensor_tensor(d["lg"][:], lg, rb0[:].unsqueeze(1).broadcast_to([P, NT, E]), ALU.add))
                else:
                    link(V.tensor_copy(d["lg"][:], lg))
                if L is L1:
                    link(V.tensor_reduce(d["s1"][:], d["lg"][:], AX.X, ALU.max))
                    V.tensor_tensor(d["lg"][:], d["lg"][:], d["s1"][:].unsqueeze(2).broadcast_to([P, NT, E]),
                                    ALU.subtract).then_inc(m["exp_in"], 1)
                    dve.wait_ge(m["exp_out"], 1)
                    link(V.tensor_reduce(d["s2"][:], d["lg"][:], AX.X, ALU.add))
                    link(V.reciprocal(d["s2"][:], d["s2"][:]))
                    link(V.tensor_tensor(d["lg"][:], d["lg"][:], d["s2"][:].unsqueeze(2).broadcast_to([P, NT, E]),
                                         ALU.mult))
                for t in range(NT):
                    ins = V.max(d["top"][:, t, :], d["lg"][:, t, :])
                link(ins)
                for t in range(NT):
                    ins = V.max_index(d["idx"][:, t, :], d["top"][:, t, :], d["lg"][:, t, :])
                link(ins)
                link(V.tensor_copy(d["idxf"][:], d["idx"][:]))
                link(V.tensor_tensor(r["oh"], iota_e[:, 0:E].unsqueeze(1).unsqueeze(1).broadcast_to([P, NT, K, E]),
                                     d["idxf"][:, :, 0:K].unsqueeze(3).broadcast_to([P, NT, K, E]), ALU.is_equal))
                with nc.allow_low_precision(reason="sums of at most one 1"):
                    V.tensor_reduce(d["m16"][:], r["oh"].rearrange("p t k e -> p t e k"), AX.X,
                                    ALU.add).then_inc(m["mask"], 1)
                if L is L0:
                    V.tensor_tensor(d["rw"][:], d["top"][:, :, 0:K], d["top"][:, :, 0:1].broadcast_to([P, NT, K]),
                                    ALU.subtract).then_inc(m["exp_in"], 1)
                else:
                    V.tensor_copy(d["rw"][:], d["top"][:, :, 0:K])
                dve.wait_ge(m["counts"], 1)
                link(V.tensor_copy(d["cnt"][0:E, :], bank[3][0:E, 0:1]))
                link(V.tensor_scalar(d["junk"][0:E, :], thr[0:E, :], d["cnt"][0:E, :], None, ALU.is_lt, ALU.add,
                                     accum_out=d["ntc"][0:E, :]))
                V.tensor_scalar(d["ntr"][0:E, :], ones16[0:E, :], d["ntc"][0:E, :], None, ALU.mult).then_inc(m["ntiles"], 1)
                dve.wait_ge(m["starts"], 1)
                link(V.tensor_copy(d["endc"][0:E, :], bank[3][0:E, 8:9]))
                V.tensor_scalar(d["cmp"][0:E, :], iota16[0:E, 0:L.tiles], d["endc"][0:E, :], None,
                                ALU.is_ge).then_inc(m["cmp"], 1)
                link(V.tensor_scalar(d["startb"][:], bank[3][:, 16:16 + E], float(P), None, ALU.mult))
                link(V.tensor_tensor(r["base"], bank[2][:, 0:NT * E].rearrange("p (t e) -> p t e", t=NT),
                                     d["startb"][:].unsqueeze(1).broadcast_to([P, NT, E]), ALU.add))
                link(V.tensor_tensor(r["pr"], r["oh"], r["base"].unsqueeze(2).broadcast_to([P, NT, K, E]), ALU.mult))
                link(V.tensor_reduce(d["slotf"][:], r["pr"], AX.X, ALU.add))
                V.tensor_copy(d["back"][:], d["slotf"][:])
                link(V.tensor_copy(d["sloti"][:], d["slotf"][:]))
                V.tensor_scalar(d["ti"][:], d["sloti"][:], 7, None, ALU.logical_shift_right)
                link(V.tensor_scalar(d["pi"][:], d["sloti"][:], P - 1, None, ALU.bitwise_and))
                V.tensor_copy(d["tf"][:], d["ti"][:])
                link(V.tensor_copy(d["pf"][:], d["pi"][:]))
                link(V.tensor_tensor(r["til1"], iota16[:, 0:L.tiles].unsqueeze(1).broadcast_to([P, NT * K, L.tiles]),
                                     d["tf"][:].rearrange("p t k -> p (t k)").unsqueeze(2).broadcast_to([P, NT * K, L.tiles]),
                                     ALU.is_equal))
                for t in range(NT):
                    w = r["til1"][:, t * K:(t + 1) * K, :]
                    V.tensor_scalar(w, w, tokid[:, t:t + 1], None, ALU.mult)
                    for k in range(K):
                        V.tensor_scalar(r["pos1"][:, t * K + k, :], iota16[:], d["pf"][:, t, k:k + 1], None,
                                        ALU.is_equal).then_inc(m["onehots"], 1)
                dve.wait_ge(m["owner"], 1)
                link(V.tensor_scalar(d["te"][:], bank[1][0:1, 0:L.tiles], float(E - 1), None, ALU.min))
                V.tensor_scalar(d["etab"][:], d["te"][:], float(L.S), float(L.stride), ALU.add,
                                ALU.mult).then_inc(m["table_e"], 1)
                dve.wait_ge(m["tokens"], 1)
                V.tensor_copy(d["tab"][:], bank[0][:, 0:L.tiles]).then_inc(m["table"], 1)

            def after_shared(L, a, b, last=False):
                q, J2, work = M[L.name]["after"], 2 * L.J, after_work[L.name]
                for n in range(a, b + 1):
                    if n < b:
                        dve.wait_ge(q["evacuated"], n + 1)
                        if n >= 2:
                            dve.wait_ge(q["ht_done"], n - 1)
                        V.tensor_tensor(hh[:, n % 2, 0:J2], sg[:, n % 2, 0:J2], bank[4 + n % 2][:, J2:2 * J2],
                                        ALU.mult).then_inc(q["h_ready"], 1)
                    if n > a:
                        t = work[n - 1][1]
                        dve.wait_ge(q["d_done"], n)
                        V.tensor_tensor(x_sb[:, t, :], x_sb[:, t, :], bank[7][:, 0:H], ALU.add).then_inc(q["added"], 1)
                        if last and work[n - 1][0] == L.S - 1:
                            dve.wait_ge(q["added"], n)
                            combine(L, t, out_ready)

            def tiles(L):
                m = M[L.name]
                J2 = 2 * L.J

                def ht_copy(s, j, early):
                    dve.wait_ge(m["ht_done"], s + 1)
                    if not early:
                        dve.wait_ge(m["d_done"], s - 1)
                    V.tensor_copy(hT[0:L.J, j % 2].rearrange("p a m -> p (a m)"),
                                  bank[4 + j % 2][0:L.J, 0:2 * P]).then_inc(m["hT_copied"], 1)

                def y_copy(s, j, first, group):
                    dve.wait_ge(m["d_done"], s + 1)
                    if not first or j >= BUFS:
                        dve.wait_ge(m["y_stored"][j % BUFS], 16 * (group * (L.unroll // BUFS) + j // BUFS))
                    V.tensor_copy(ysb[:, j % BUFS, :], bank[6 + j % 2][:, 0:H]).then_inc(m["y_copied"], 1)

                def turn(base, group, first, last):
                    for j in range(L.unroll):
                        s = base + j
                        if not (first and j == 0):
                            ht_copy(s - 1, j - 1, first and j - 1 < 2)
                        dve.wait_ge(m["sg_ready"], s + 1)
                        if not first or j >= 2:
                            dve.wait_ge(m["ht_done"], s - 1)
                        V.tensor_tensor(hh[:, j % 2, 0:J2], sg[:, j % 2, 0:J2], bank[2 + j % 2][:, J2:2 * J2],
                                        ALU.mult).then_inc(m["h_ready"], 1)
                        if not (first and j == 0):
                            y_copy(s - 1, j - 1, first, group)
                    if last:
                        ht_copy(base + L.unroll - 1, L.unroll - 1, False)
                        y_copy(base + L.unroll - 1, L.unroll - 1, False, group)

                turns(dve, L, turn)

            def combine(L, t, ready):
                m, d, rows = M[L.name], small[L.name], back_rows[L.name]
                dve.wait_ge(rows_back[t], rows_in[L.name])
                for k in range(L.K):
                    ins = V.scalar_tensor_tensor(out=x_sb[:, t, :], in0=rows[:, t, k, :], scalar=d["rw"][:, t, k:k + 1],
                                                 in1=x_sb[:, t, :], op0=ALU.mult, op1=ALU.add)
                    if k < L.K - 1:
                        link(ins)
                ins.then_inc(ready, 1)

            layernorm(range(NT), M["m0"]["xn_ready"])
            routing(L0)
            after_shared(L0, 0, n_mid["m0"])
            tiles(L0)
            d = small["m0"]
            dve.wait_ge(M["m0"]["exp_out"], 1)
            link(V.tensor_reduce(d["s2"][:], d["rw"][:], AX.X, ALU.add))
            link(V.reciprocal(d["s2"][:], d["s2"][:]))
            link(V.tensor_scalar(d["s2"][:], d["s2"][:], ROUTED_SCALE, None, ALU.mult))
            link(V.tensor_tensor(d["rw"][:], d["rw"][:], d["s2"][:].unsqueeze(2).broadcast_to([P, NT, L0.K]), ALU.mult))

            def head_max(g):
                dve.wait_ge(s_done, g + 1)
                if g >= 4:
                    dve.wait_ge(p_raw, 2 * g - 6)
                V.tensor_reduce(small["nm"][:, g % 4, :], bank[g % 4][:].rearrange("p (q k) -> p q k", q=2),
                                AX.X, ALU.max, negate=True).then_inc(nm_ready, 1)

            def head_inverse(g):
                dve.wait_ge(p_raw, 2 * g + 2)
                if g >= 4:
                    dve.wait_ge(p_ready, g - 3)
                if g >= ALONE + 4:
                    dve.wait_ge(p1_ready, g - 3 - ALONE)
                V.reciprocal(small["rinv"][:, g % 4, :], small["rsum"][:, g % 4, :]).then_inc(rinv_ready, 1)
                dve.wait_ge(rinv_ready, g + 1)
                if g < ALONE:
                    V.tensor_scalar(pr_sb[:, g % 4, 1, :], pr_sb[:, g % 4, 1, :], small["rinv"][:, g % 4, 1:2],
                                    None, ALU.mult).then_inc(p2_ready, 1)

            def tile_out(t):
                dve.wait_ge(av_done, HPT * (t + 1))
                V.scalar_tensor_tensor(out=x_sb[:, t, :], in0=bank[6 + t % 2][:, 0:H], scalar=gamma_sb[:], in1=x_sb[:, t, :],
                                       op0=ALU.mult, op1=ALU.add).then_inc(x3_ready, 1)

            def take(t):
                combine(L0, t, x2_ready)
                dve.wait_ge(x2_ready, t + 1)

            dve.wait_ge(small_in, 64)
            dve.wait_ge(M["m0"]["early"]["added"], n_early["m0"])
            dve.wait_ge(M["m0"]["after"]["added"], n_mid["m0"])
            def queries(tiles, deviations=False):
                if not deviations:
                    link(statistics(tiles))
                    inverse_deviation(V, link, tiles, SCALE)
                link(normalise(tiles))
                for t in tiles:
                    if t >= 2:
                        dve.wait_ge(q3_stored, 16 * HPT * (t - 1))
                    ins = V.tensor_copy(q3[:, t % 2, 0], xn[:, t, :])
                link(ins)
                for t in tiles:
                    ins = V.tensor_tensor(xn[:, t, :], xn[:, t, :], q3[:, t % 2, 0], ALU.subtract)
                link(ins)
                for t in tiles:
                    ins = V.tensor_copy(q3[:, t % 2, 1], xn[:, t, :])
                link(ins)
                for t in tiles:
                    V.tensor_tensor(q3[:, t % 2, 2], xn[:, t, :], q3[:, t % 2, 1], ALU.subtract).then_inc(q3_ready, 1)

            take(0)
            queries([0])
            take(1)
            queries([1])
            take(2)
            take(3)
            between = {0: [lambda: queries([2, 3])]}
            for t in range(4, NT, 2):
                at = HPT * t - 11
                between.setdefault(at - 2, []).append(lambda t=t: take(t))
                between.setdefault(at, []).append(lambda t=t: take(t + 1))
            for g in range(3):
                head_max(g)
            for g in range(2):
                head_inverse(g)
            for g in range(nheads):
                for work in between.get(g, []):
                    work()
                if g in by_pool:
                    statistics(by_pool[g][0]).then_inc(stats_ready, 1)
                if g - 3 in by_pool:
                    group_tiles, scale = by_pool[g - 3]
                    dve.wait_ge(rstd_ready, sum(k <= g - 3 for k in by_pool))
                    if scale == SCALE:
                        queries(group_tiles, True)
                    else:
                        normalise(group_tiles, M["m1"]["xn_ready"])
                if g + 3 < nheads:
                    head_max(g + 3)
                if g + 2 < nheads:
                    head_inverse(g + 2)
                if g % HPT == 1 and g > HPT:
                    t = g // HPT - 1
                    tile_out(t)
                    dve.wait_ge(x3_ready, t + 1)
            tile_out(NT - 1)
            dve.wait_ge(x3_ready, NT)
            layernorm([NT - 2, NT - 1], M["m1"]["xn_ready"])
            routing(L1)
            after_shared(L1, 0, n_mid["m1"])
            tiles(L1)

            dve.wait_ge(M["m1"]["early"]["added"], n_early["m1"])
            after_shared(L1, n_mid["m1"], len(after_work["m1"]), True)

        @block.tensor
        def _(pe):
            T = nc.tensor
            pe.wait_ge(consts, 8)
            pe.wait_ge(amc_ready, 1)
            T.transpose(bank[2][0:16, 0:P], amc[:], ident[:]).then_inc(amcT_done, 1)
            pe.wait_ge(diag_ready, 1)
            T.matmul(bank[3][:, 0:16], ones32[0:16, :], diag[0:16, :], start=True, stop=True).then_inc(amb_done, 1)
            for i in range(2):
                pe.wait_ge(xq_ready, i + 1)
                b16 = bank[i][:].bitcast(BF16)
                for a in range(8):
                    ins = T.transpose(b16[:, a * P:(a + 1) * P], qx[:, (8 * i + a) * P:(8 * i + a + 1) * P], ident16[:])
                ins.then_inc(xqT_done, 1)
                pe.wait_ge(wq_ready, 1)
                pe.wait_ge(xqT_sb, i + 1)
                for t in range(4 * i, 4 * i + 4):
                    if t >= 2:
                        pe.wait_ge(x1_ready, t - 1)
                    for k in range(C):
                        ins = T.matmul(bank[4 + t % 2][:, k * H:(k + 1) * H], xqT[:, t, k, :], wq[:, t // 2, k, :],
                                       start=True, stop=True)
                    ins.then_inc(xp_done, 1)

            def shared_steps(L, part, a, b, start, end):
                q = M[L.name][part]
                work = (early_work if part == "early" else after_work)[L.name]
                J2 = 2 * L.J
                for n in range(start, end):
                    if n > a:
                        pe.wait_ge(q["h_ready"], n)
                        if n >= 2:
                            pe.wait_ge(q["hT_copied"], n - 1)
                        for h in range(2):
                            ins = T.transpose(bank[6][0:L.J, h * P:(h + 1) * P], hh[:, (n - 1) % 2, h * L.J:(h + 1) * L.J],
                                              ident[:])
                        ins.then_inc(q["ht_done"], 1)
                    if n < b:
                        i, t = work[n]
                        if n >= 2:
                            pe.wait_ge(q["evacuated"], n - 1)
                            pe.wait_ge(q["h_ready"], n - 1)
                        for c in range(C):
                            at = i * L.stride + c * 2 * J2
                            ins = T.matmul(bank[4 + n % 2][:, 0:2 * J2], RS[L.name]["xT"][:, t, c, :],
                                           arena[:, at:at + 2 * J2], start=(c == 0), stop=(c == C - 1))
                        ins.then_inc(q["g_done"], 1)
                    if n > a:
                        pe.wait_ge(q["hT_copied"], n)
                        if n >= 2:
                            pe.wait_ge(q["y_copied" if part == "early" else "added"], n - 1)
                        elif part == "after":
                            pe.wait_ge(M[L.name]["early"]["y_copied"], n_early[L.name])
                        for h in range(2):
                            at = work[n - 1][0] * L.stride + L.gu + h * H
                            ins = T.matmul(bank[7][:, 0:H], hT[0:L.J, (n - 1) % 2, h, :], arena[0:L.J, at:at + H],
                                           start=(h == 0), stop=(h == 1))
                        ins.then_inc(q["d_done"], 1)

            def turn_rows(L, i):
                m = M[L.name]
                pe.wait_ge(m["xn_ready"], 2 * i + 2)
                if i >= 2:
                    pe.wait_ge(m["rt_Tsb"], i - 1)
                for t in (2 * i, 2 * i + 1):
                    for c in range(C):
                        at = ((t % 2) * C + c) * P
                        ins = T.transpose(bank[i % 2][:, at:at + P], xn[:, t, c * P:(c + 1) * P], ident[:])
                ins.then_inc(m["rt_T"], 1)

            def routing(L, rw, w_in, turned=0):
                m, d, r = M[L.name], small[L.name], RS[L.name]
                E, K = L.E, L.K

                for i in range(turned, 2):
                    turn_rows(L, i)
                for i in range(NT // 2):
                    if i >= 1 and i + 1 < NT // 2:
                        turn_rows(L, i + 1)
                    pe.wait_ge(m["rt_Tsb"], i + 1)
                    for t in (2 * i, 2 * i + 1):
                        o = bank[2][:, t * E:(t + 1) * E]
                        for c in range(C):
                            ins = T.matmul(o, r["xT"][:, t, c, :], rw[:, c, :], start=(c == 0), stop=(c == C - 1))
                        ins.then_inc(m["logits"], 1)
                N = n_early[L.name]
                pe.wait_ge(*w_in)
                shared_steps(L, "early", 0, N, 0, 1)
                pe.wait_ge(m["mask"], 1)
                for t in range(NT):
                    ins = T.matmul(bank[3][0:E, 0:1], d["m16"][:, t, :], ones16[:, 0:1], start=(t == 0), stop=(t == NT - 1))
                ins.then_inc(m["counts"], 1)
                T.matmul(bank[2][:, 0:NT * E], tri16[:], d["m16"][:].rearrange("p t e -> p (t e)"), start=True, stop=False,
                         skip_group_check=True)
                for t in range(NT - 1):
                    n = NT - 1 - t
                    T.matmul(bank[2][:, (t + 1) * E:NT * E], ones16[:],
                             d["m16"][:, t:t + 1, :].broadcast_to([P, n, E]), start=False, stop=(t == NT - 2),
                             skip_group_check=True)
                pe.wait_ge(m["ntiles"], 1)
                T.matmul(bank[3][:, 16:16 + E], d["ntr"][0:E, :], tri16[0:E, 0:E], start=True, stop=True)
                T.matmul(bank[3][0:E, 8:9], tri_in16[0:E, 0:E], d["ntr"][0:E, 0:1], start=True, stop=True).then_inc(m["starts"], 1)
                pe.wait_ge(m["cmp"], 1)
                T.matmul(bank[1][0:1, 0:L.tiles], ones16[0:E, 0:1], d["cmp"][0:E, :], start=True,
                         stop=True).then_inc(m["owner"], 1)
                shared_steps(L, "early", 0, N, 1, N + 1)
                for a in range(NT * K):
                    pe.wait_ge(m["onehots"], a + 1)
                    ins = T.matmul(bank[0][:, 0:L.tiles], r["pos1"][:, a, :], r["til1"][:, a, :], start=(a == 0),
                                   stop=(a == NT * K - 1))
                ins.then_inc(m["tokens"], 1)
                shared_steps(L, "after", 0, n_mid[L.name], 0, n_mid[L.name] + 1)

            def tiles(L):
                m, d = M[L.name], small[L.name]
                J2 = 2 * L.J
                top = (L.S + L.E - 1) * L.stride
                pe.wait_ge(m["table_e"], 1)

                def weights_of(s):
                    return pe.value_load(d["etab"][0:1, bass.ds(s, 1)], min_val=0, max_val=top)

                def turn_in(s, j, group, early):
                    pe.wait_ge(m["xg_in"][j % BUFS], 16 * (group * (L.unroll // BUFS) + j // BUFS + 1))
                    if not early:
                        pe.wait_ge(m["xT_copied"], s - 1)
                    for c in range(C):
                        ins = T.transpose(bank[j % 2][:, c * P:(c + 1) * P], xg[:, j % BUFS, c * P:(c + 1) * P], ident[:])
                    ins.then_inc(m["t_done"], 1)

                def gate_up(j, c, off):
                    return T.matmul(bank[2 + j % 2][:, 0:2 * J2], xT[:, j % 2, c, :],
                                    arena[:, bass.ds(off + c * 2 * J2, 2 * J2)], start=(c == 0), stop=(c == C - 1))

                def turn_h(s, j, early):
                    pe.wait_ge(m["h_ready"], s + 1)
                    if not early:
                        pe.wait_ge(m["hT_copied"], s - 1)
                    for a in range(2):
                        ins = T.transpose(bank[4 + j % 2][0:L.J, a * P:(a + 1) * P], hh[:, j % 2, a * L.J:(a + 1) * L.J],
                                          ident[:])
                    ins.then_inc(m["ht_done"], 1)

                def down(s, j, off, early):
                    pe.wait_ge(m["hT_copied"], s + 1)
                    if not early:
                        pe.wait_ge(m["y_copied"], s - 1)
                    for a in range(2):
                        ins = T.matmul(bank[6 + j % 2][:, 0:H], hT[0:L.J, j % 2, a, :],
                                       arena[0:L.J, bass.ds(off + L.gu + a * H, H)], start=(a == 0), stop=(a == 1))
                    ins.then_inc(m["d_done"], 1)

                def turn(base, group, first, last):
                    before = None if first else weights_of(base - 1)
                    off = weights_of(base)
                    for j in range(L.unroll):
                        s = base + j
                        early = first and j < 2
                        pe.wait_ge(m["xT_copied"], s + 1)
                        if not early:
                            pe.wait_ge(m["h_ready"], s - 1)
                        gate_up(j, 0, off)
                        if before is not None:
                            turn_h(s - 1, j - 1, first and j - 1 < 2)
                        if not (last and j == L.unroll - 1):
                            turn_in(s + 1, j + 1, group, first and j + 1 < 2)
                        gate_up(j, 1, off).then_inc(m["g_done"], 1)
                        after = weights_of(s + 1) if j + 1 < L.unroll else None
                        if before is not None:
                            down(s - 1, j - 1, before, first and j - 1 < 2)
                        before, off = off, after
                    if last:
                        turn_h(base + L.unroll - 1, L.unroll - 1, False)
                        down(base + L.unroll - 1, L.unroll - 1, before, False)

                turn_in(0, 0, 0, True)
                turns(pe, L, turn)

            pe.wait_ge(small_in, 64)
            routing(L0, rw0, (w_shared, 32))
            pe.wait_ge(w_early, 32 * -(-(L0.E - LATE) // EARLY))
            pe.wait_ge(w_late, 64)
            tiles(L0)


            Q_LOADS, K_LOADS = (16 * sum(2 if p[i][0] > p[i][1] else 1 for p in QK_PARTS) for i in range(2))
            KV = 16 + K_LOADS + 16

            def scores(g):
                t = g // HPT
                pe.wait_ge(batch_in[t // 2], KV)
                pe.wait_ge(qs_in[t % 2], Q_LOADS * (t // 2 + 1))
                if g >= 4:
                    pe.wait_ge(p_raw, 2 * g - 6)
                for q in range(2):
                    for s_ in range(2):
                        ins = T.matmul(bank[g % 4][:, q * H:(q + 1) * H], qs[:, t % 2, s_, g % HPT, q * P:(q + 1) * P],
                                       ks[:, s_, g, :], start=(s_ == 0), stop=(s_ == 1))
                ins.then_inc(s_done, 1)

            def turn_p(g):
                pe.wait_ge(p_ready, g + 1)
                if g < ALONE:
                    pe.wait_ge(p2_ready, g + 1)
                if g >= ALONE:
                    pe.wait_ge(p1_ready, g + 1 - ALONE)
                if g >= 2:
                    pe.wait_ge(pT_ready, g - 1)
                for k in range(2):
                    for q in range(2):
                        ins = T.transpose(bank[4 + g % 2][:, (2 * k + q) * P:(2 * k + q + 1) * P],
                                          pr_sb[:, g % 4, q, k * P:(k + 1) * P], ident[:])
                ins.then_inc(tp_done, 1)

            def values(g):
                t, r0 = g // HPT, (g % HPT) * HEAD
                pe.wait_ge(batch_in[t // 2], KV)
                pe.wait_ge(pT_ready, g + 1)
                if t >= 2:
                    pe.wait_ge(x3_ready, t - 1)
                for k in range(2):
                    row = (t % 2) * P + r0
                    ins = T.matmul(bank[6 + t % 2][r0:r0 + HEAD, 0:H], vT[:, t // 2, k, row:row + HEAD],
                                   pT_sb[:, g % 2, k, :], start=(k == 0), stop=(k == 1), tile_position=(0, r0))
                ins.then_inc(av_done, 1)

            for g in range(3):
                scores(g)
            for g in range(nheads + 1):
                if g + 3 < nheads:
                    scores(g + 3)
                if g < nheads:
                    turn_p(g)
                if g >= 1:
                    values(g - 1)
                if g >= nheads - 1:
                    pe.wait_ge(p_raw, 2 * (nheads - 2))
                    turn_rows(L1, g - (nheads - 1))
            routing(L1, rw1, (w1_in, 96), 2)
            tiles(L1)
            shared_steps(L1, "after", n_mid["m1"], len(after_work["m1"]), n_mid["m1"], len(after_work["m1"]) + 1)


def kernel(**inputs):
    import numpy as np
    import concourse.bacc as bacc
    from concourse.bass_utils import run_bass_kernel_spmd

    a = {k: np.asarray(v) for k, v in inputs.items()}

    def chunks(w):
        n, h = w.shape
        return np.ascontiguousarray(w.T.reshape(h // P, P, n).transpose(1, 0, 2))

    def experts(gate, up, down):
        e, i, h = gate.shape
        gu = np.concatenate([gate, up], axis=1).transpose(2, 0, 1).reshape(h // P, P, e, 2 * i).transpose(1, 2, 0, 3)
        dn = down.transpose(2, 0, 1).reshape(2, i // 2, e, h).transpose(1, 2, 0, 3)
        return np.ascontiguousarray(gu.reshape(P, e, -1)), np.ascontiguousarray(dn.reshape(i // 2, e, -1))

    def halves(w, i, axis):
        return np.stack(np.split(w, w.shape[axis] // i, axis=axis))

    i0 = a["L0_ffn_gate_w"].shape[1]
    gu0, dn0 = experts(*(np.concatenate([halves(a["L0_ffn_shared_" + n], i0, ax), a["L0_ffn_" + n]])
                         for n, ax in (("gate_w", 0), ("up_w", 0), ("down_w", 1))))
    i1 = a["L1_ffn_w1"].shape[1]
    gu1, dn1 = experts(*(np.concatenate([halves(a["L1_ffn_s" + n], i1, ax), a["L1_ffn_" + n]])
                         for n, ax in (("w1", 0), ("w2", 0), ("w3", 1))))
    x = a["x"]
    H = x.shape[2]
    arrays = {
        "x": x.reshape(-1, P, H), "ctx": a["ctx_2048"], "ctxT": np.ascontiguousarray(a["ctx_2048"].transpose(0, 2, 1)),
        "router_w0": chunks(a["L0_ffn_router_w"]), "router_b0": a["L0_ffn_router_b"].reshape(1, -1),
        "w_gu0": gu0, "w_dn0": dn0, "gamma": a["L1_xattn_gamma"].reshape(1, 1),
        "router_w1": chunks(a["L1_ffn_gate_w"]), "w_gu1": gu1, "w_dn1": dn1,
    }
    arrays = {k: np.ascontiguousarray(v) for k, v in arrays.items()}
    nc = bacc.Bacc("TRN2", target_bir_lowering=False, num_devices=1)
    args = [nc.dram_tensor(n, v.shape, mybir.dt.from_np(v.dtype), kind="ExternalInput").ap() for n, v in arrays.items()]
    out = nc.dram_tensor("out", arrays["x"].shape, F32, kind="ExternalOutput").ap()
    mk_xattn_ffn(nc, *args, out)
    r = run_bass_kernel_spmd(nc, [arrays], core_ids=[0])
    return r.results[0]["out"].reshape(x.shape)
```
